# Optimizing a Trainium2 kernel written in Bass

```python
import numpy as np
import jax
import jax.numpy as jnp

def _softmax(x, axis=-1):
    return jax.nn.softmax(x, axis=axis)

def _gelu(x):
    return jax.nn.gelu(x, approximate=True)

def _silu(x):
    return jax.nn.silu(x)

def _sigmoid(x):
    return jax.nn.sigmoid(x)

def _layernorm(x, axis=-1, eps=1e-05):
    m = jnp.mean(x, axis=axis, keepdims=True)
    v = jnp.var(x, axis=axis, keepdims=True)
    return (x - m) / jnp.sqrt(v + eps)

def _scatter_add(tgt, idx, src, axis=0):
    return tgt.at[idx].add(src)

def _segment_sum(src, seg, n):
    return jax.ops.segment_sum(src, seg, n)
kernel_name = 'mk_conv_seq_d2_conv_nhwc256_r2_12be40'

def setup_inputs(seed: int=0):
    np.random.seed(seed)
    _w = jnp.asarray

    def _rec_inputs():
        import jax
        import jax.numpy as jnp
        _gk = jax.random.key(seed)
        x = -0.0003929 + 0.9999 * jax.random.normal(jax.random.fold_in(_gk, 1), (16, 32, 32, 128), jnp.float32)
        return x
    x = _rec_inputs()

    def _L0_conv_setup():
        import math
        import jax, jax.numpy as jnp
        import numpy as np
        B, H, W, C = (16, 32, 32, 128)
        _POS = [(-1, -1), (-1, 0), (-1, 1), (0, -1), (0, 0), (0, 1), (1, -1), (1, 0), (1, 1)]

        def _local_attn(hn, w_qkv, b_qkv):
            Bb, Hh, Ww, Cc = hn.shape
            qkv = jnp.einsum('bhwc,dc->bhwd', hn, w_qkv) + b_qkv
            q, k, v = jnp.split(qkv, 3, axis=-1)
            kp = jnp.pad(k, ((0, 0), (1, 1), (1, 1), (0, 0)))
            vp = jnp.pad(v, ((0, 0), (1, 1), (1, 1), (0, 0)))
            scale = 1.0 / math.sqrt(Cc)
            scores = jnp.stack([(q * kp[:, 1 + dy:1 + dy + Hh, 1 + dx:1 + dx + Ww, :]).sum(-1) for dy, dx in _POS], axis=-1) * scale
            w = jax.nn.softmax(scores, axis=-1)
            out = jnp.zeros_like(v)
            for i, (dy, dx) in enumerate(_POS):
                out = out + w[..., i:i + 1] * vp[:, 1 + dy:1 + dy + Hh, 1 + dx:1 + dx + Ww, :]
            return out
        key = jax.random.key(seed)
        ks = jax.random.split(key, 6)
        return {'h': jax.random.normal(ks[0], (B, H, W, C), jnp.float32), 'w_perc': jax.random.normal(ks[1], (3 * C, 1, 3, 3), jnp.float32) * 0.1, 'b_perc': jnp.zeros((3 * C,), jnp.float32), 'w_up1': jax.random.normal(ks[2], (2 * C, 3 * C, 1, 1), jnp.float32) * 0.02, 'b_up1': jnp.zeros((2 * C,), jnp.float32), 'w_up2': jax.random.normal(ks[3], (C, 2 * C, 1, 1), jnp.float32) * 0.02, 'b_up2': jnp.zeros((C,), jnp.float32), 'w_qkv': jax.random.normal(ks[4], (3 * C, C), jnp.float32) * 0.02, 'b_qkv': jnp.zeros((3 * C,), jnp.float32)}
    _L0_conv_all = _L0_conv_setup()
    _L0_conv_in = {k: v for k, v in _L0_conv_all.items() if k in ('w_perc', 'b_perc', 'w_up1', 'b_up1', 'w_up2', 'b_up2', 'w_qkv', 'b_qkv')}
    del _L0_conv_all

    def _L1_conv_setup():
        import jax, jax.numpy as jnp
        import numpy as np
        UNITS = 128
        GROUPS = 8
        EPS = 0.001

        def group_norm(x, gamma, beta, groups=GROUPS, eps=EPS):
            B, H, W, C = x.shape
            xg = x.reshape(B, H, W, groups, C // groups)
            mean = xg.mean(axis=(1, 2, 4), keepdims=True)
            var = xg.var(axis=(1, 2, 4), keepdims=True)
            xn = (xg - mean) * jax.lax.rsqrt(var + eps)
            xn = xn.reshape(B, H, W, C)
            return xn * gamma + beta
        key = jax.random.key(seed)
        ks = jax.random.split(key, 10)
        B, H, W, C = (4, 32, 32, UNITS)
        s = 1.0 / np.sqrt(C)
        x = jax.random.normal(ks[0], (B, H, W, C), dtype=jnp.float32)
        return {'x': x, 'gamma': jnp.ones((C,), jnp.float32), 'beta': jnp.zeros((C,), jnp.float32), 'Wq': jax.random.uniform(ks[1], (C, C), jnp.float32, -s, s), 'bq': jnp.zeros((C,), jnp.float32), 'Wk': jax.random.uniform(ks[2], (C, C), jnp.float32, -s, s), 'bk': jnp.zeros((C,), jnp.float32), 'Wv': jax.random.uniform(ks[3], (C, C), jnp.float32, -s, s), 'bv': jnp.zeros((C,), jnp.float32), 'Wp': jax.random.uniform(ks[4], (C, C), jnp.float32, -1e-05, 1e-05), 'bp': jnp.zeros((C,), jnp.float32)}
    _L1_conv_all = _L1_conv_setup()
    _L1_conv_in = {k: v for k, v in _L1_conv_all.items() if k in ('gamma', 'beta', 'Wq', 'bq', 'Wk', 'bk', 'Wv', 'bv', 'Wp', 'bp')}
    del _L1_conv_all
    return {'x': x, 'L0_conv_w_perc': _L0_conv_in['w_perc'], 'L0_conv_b_perc': _L0_conv_in['b_perc'], 'L0_conv_w_up1': _L0_conv_in['w_up1'], 'L0_conv_b_up1': _L0_conv_in['b_up1'], 'L0_conv_w_up2': _L0_conv_in['w_up2'], 'L0_conv_b_up2': _L0_conv_in['b_up2'], 'L0_conv_w_qkv': _L0_conv_in['w_qkv'], 'L0_conv_b_qkv': _L0_conv_in['b_qkv'], 'L1_conv_gamma': _L1_conv_in['gamma'], 'L1_conv_beta': _L1_conv_in['beta'], 'L1_conv_Wq': _L1_conv_in['Wq'], 'L1_conv_bq': _L1_conv_in['bq'], 'L1_conv_Wk': _L1_conv_in['Wk'], 'L1_conv_bk': _L1_conv_in['bk'], 'L1_conv_Wv': _L1_conv_in['Wv'], 'L1_conv_bv': _L1_conv_in['bv'], 'L1_conv_Wp': _L1_conv_in['Wp'], 'L1_conv_bp': _L1_conv_in['bp']}

def reference(x, L0_conv_w_perc, L0_conv_b_perc, L0_conv_w_up1, L0_conv_b_up1, L0_conv_w_up2, L0_conv_b_up2, L0_conv_w_qkv, L0_conv_b_qkv, L1_conv_gamma, L1_conv_beta, L1_conv_Wq, L1_conv_bq, L1_conv_Wk, L1_conv_bk, L1_conv_Wv, L1_conv_bv, L1_conv_Wp, L1_conv_bp):
    import jax
    import jax.numpy as jnp

    def _L0_conv_ref(h, w_perc, b_perc, w_up1, b_up1, w_up2, b_up2, w_qkv, b_qkv):
        import math
        import jax, jax.numpy as jnp
        import numpy as np
        B, H, W, C = (16, 32, 32, 128)
        _POS = [(-1, -1), (-1, 0), (-1, 1), (0, -1), (0, 0), (0, 1), (1, -1), (1, 0), (1, 1)]

        def _local_attn(hn, w_qkv, b_qkv):
            Bb, Hh, Ww, Cc = hn.shape
            qkv = jnp.einsum('bhwc,dc->bhwd', hn, w_qkv) + b_qkv
            q, k, v = jnp.split(qkv, 3, axis=-1)
            kp = jnp.pad(k, ((0, 0), (1, 1), (1, 1), (0, 0)))
            vp = jnp.pad(v, ((0, 0), (1, 1), (1, 1), (0, 0)))
            scale = 1.0 / math.sqrt(Cc)
            scores = jnp.stack([(q * kp[:, 1 + dy:1 + dy + Hh, 1 + dx:1 + dx + Ww, :]).sum(-1) for dy, dx in _POS], axis=-1) * scale
            w = jax.nn.softmax(scores, axis=-1)
            out = jnp.zeros_like(v)
            for i, (dy, dx) in enumerate(_POS):
                out = out + w[..., i:i + 1] * vp[:, 1 + dy:1 + dy + Hh, 1 + dx:1 + dx + Ww, :]
            return out
        Cc = h.shape[-1]
        x = jnp.transpose(h, (0, 3, 1, 2))
        perceived = jax.lax.conv_general_dilated(x, w_perc, window_strides=(1, 1), padding='SAME', feature_group_count=Cc, dimension_numbers=('NCHW', 'OIHW', 'NCHW')) + b_perc[None, :, None, None]
        hid = jnp.einsum('bphw,dp->bdhw', perceived, w_up1[:, :, 0, 0]) + b_up1[None, :, None, None]
        hid = jax.nn.gelu(hid, approximate=False)
        dx = jnp.einsum('bdhw,cd->bchw', hid, w_up2[:, :, 0, 0]) + b_up2[None, :, None, None]
        x_new = x + dx
        h_new = jnp.transpose(x_new, (0, 2, 3, 1))
        h_attn = _local_attn(h_new, w_qkv, b_qkv)
        return h_new + h_attn

    def _L1_conv_ref(x, gamma, beta, Wq, bq, Wk, bk, Wv, bv, Wp, bp):
        import jax, jax.numpy as jnp
        import numpy as np
        UNITS = 128
        GROUPS = 8
        EPS = 0.001

        def group_norm(x, gamma, beta, groups=GROUPS, eps=EPS):
            B, H, W, C = x.shape
            xg = x.reshape(B, H, W, groups, C // groups)
            mean = xg.mean(axis=(1, 2, 4), keepdims=True)
            var = xg.var(axis=(1, 2, 4), keepdims=True)
            xn = (xg - mean) * jax.lax.rsqrt(var + eps)
            xn = xn.reshape(B, H, W, C)
            return xn * gamma + beta
        B, H, W, C = x.shape
        scale = jnp.float32(C) ** (-0.5)
        xn = group_norm(x, gamma, beta)
        n = H * W
        xf = xn.reshape(B, n, C)
        q = xf @ Wq + bq
        k = xf @ Wk + bk
        v = xf @ Wv + bv
        attn = jnp.einsum('bnc,bmc->bnm', q, k) * scale
        attn = jax.nn.softmax(attn, axis=-1)
        out = jnp.einsum('bnm,bmc->bnc', attn, v)
        out = out @ Wp + bp
        return xn + out.reshape(B, H, W, C)

    def _gn(v, G=32, eps=1e-05):
        B_, H_, W_, C_ = v.shape
        g = v.reshape(B_, H_, W_, G, C_ // G)
        m = jnp.mean(g, axis=(1, 2, 4), keepdims=True)
        s = jnp.var(g, axis=(1, 2, 4), keepdims=True)
        return ((g - m) / jnp.sqrt(s + eps)).reshape(v.shape)

    def _ln_c(v, eps=1e-06):
        m = jnp.mean(v, axis=-1, keepdims=True)
        s = jnp.var(v, axis=-1, keepdims=True)
        return (v - m) / jnp.sqrt(s + eps)

    def _ln_t(v, eps=1e-05):
        m = jnp.mean(v, axis=-1, keepdims=True)
        s = jnp.var(v, axis=-1, keepdims=True)
        return (v - m) / jnp.sqrt(s + eps)

    def _to_tokens(v):
        B_, H_, W_, C_ = v.shape
        return v.reshape(B_, H_ * W_, C_)

    def _from_tokens(t, like):
        return t.reshape(like.shape)
    x = _L0_conv_ref(x, L0_conv_w_perc, L0_conv_b_perc, L0_conv_w_up1, L0_conv_b_up1, L0_conv_w_up2, L0_conv_b_up2, L0_conv_w_qkv, L0_conv_b_qkv)
    x = _L1_conv_ref(x, L1_conv_gamma, L1_conv_beta, L1_conv_Wq, L1_conv_bq, L1_conv_Wk, L1_conv_bk, L1_conv_Wv, L1_conv_bv, L1_conv_Wp, L1_conv_bp)
    return x

_drawn_inputs = setup_inputs


def setup_inputs(seed=0):
    import zlib

    import numpy as np

    out = dict(_drawn_inputs(seed))
    spreads = {'L0_conv_b_perc': (0.0, 0.8),
     'L0_conv_b_up1': (0.0, 0.546),
     'L0_conv_b_up2': (0.0, 0.1),
     'L0_conv_b_qkv': (0.0, 0.1),
     'L1_conv_gamma': (1.0, 0.2),
     'L1_conv_beta': (0.0, 0.1),
     'L1_conv_bq': (0.0, 2.0),
     'L1_conv_bk': (0.0, 0.8),
     'L1_conv_bv': (0.0, 2.0),
     'L1_conv_bp': (0.0, 0.1)}
    factors = {'L0_conv_w_perc': 3.051,
     'L0_conv_w_up1': 2.851,
     'L1_conv_Wq': 64.0,
     'L1_conv_Wk': 64.0,
     'L1_conv_Wv': 64.0,
     'L1_conv_Wp': 64.0}
    for name, (base, spread) in spreads.items():
        noise = np.random.default_rng([zlib.crc32(name.encode()), seed]).standard_normal(out[name].shape)
        drawn = base * np.exp(spread * noise) if base else spread * noise
        out[name] = jnp.asarray(drawn.astype(out[name].dtype))
    for name, factor in factors.items():
        out[name] = (out[name] * factor).astype(out[name].dtype)
    return out
```

```python
from contextlib import ExitStack

import concourse.bass as bass
from concourse import mybir

F32 = mybir.dt.float32
F32R = mybir.dt.float32r
ALU = mybir.AluOpType
ACT = mybir.ActivationFunctionType
AX = mybir.AxisListType

B, H, W, C = 16, 32, 32, 128
PIX = H * W
TILES = PIX // 128
HALF = PIX // 2
ROWS = H // 2
HP, WP = H + 2, W + 2
TAPS = 9
WIN = 6 * WP
D = 2 * C
GROUP = C // 8
EPS = 1e-3
SCALE = float(C) ** -0.5
MASKED = -1e30
CONST_W = 128 + WIN + 128


class Count:

    def __init__(self, handle, per_image, unit=1):
        self.handle, self.per_image, self.unit = handle, per_image, unit

    def after(self, n, e):
        value = n * (self.per_image * self.unit) + (e + 1) * self.unit
        return self.handle, max(value, 0) if isinstance(value, int) else value


BANK_PLAN = [
    ("xt", 0, 0), ("xt", 1, 1), ("xbt", 0, 2), ("xbt", 1, 3), ("as", 0, 0), ("conv", 0, 2),
    ("at", 0, 1), ("as", 1, 0), ("conv", 1, 3),
    ("av", 0, 1), ("at", 1, 0), ("as", 2, 1), ("conv", 2, 2),
    ("av", 1, 0), ("at", 2, 1), ("as", 3, 0), ("up2", 0, 3), ("pv", 0, 1),
    ("av", 2, 0), ("at", 3, 3), ("ft", 0, 2), ("conv", 3, 1),
    ("av", 3, 0), ("q", 0, 2), ("k", 0, 3), ("v", 0, 0), ("up2", 1, 2),
    ("gn", 0, 3),
    ("q", 1, 0), ("k", 1, 1), ("v", 1, 2), ("pv", 1, 3),
    ("qq", 0, 0), ("qq", 1, 1), ("kk", 0, 2), ("kk", 1, 0), ("ft", 1, 1), ("vv", 0, 2), ("vv", 1, 3),
]
BANK_OF = {(u, e): bank for u, e, bank in BANK_PLAN}
STAGE_OF = dict(xt=1, conv=1, up2=1, q=1, k=1, v=1, av=2, at=2, gn=2, qq=2, kk=2, vv=2, xbt=3, pv=3, ft=3)
STAGE_OF["as"] = 2


class Turn:

    def __init__(self, it):
        self.it = it
        self.a, self.b, self.c = it, it + 1, it + 2
        self.fixed = isinstance(it, int)

    def active(self, stage, back=0):
        if not self.fixed:
            return True
        return 0 <= self.it - back + 3 - stage < B

    def previous_user(self, user, e):
        at = [(u, x) for u, x, _ in BANK_PLAN].index((user, e))
        before = [(u, x, 0) for u, x, b in BANK_PLAN[:at] if b == BANK_OF[user, e]][::-1]
        whole = [(u, x) for u, x, b in BANK_PLAN if b == BANK_OF[user, e]][::-1]
        for back in range(1, 4):
            before += [(u, x, back) for u, x in whole]
        for u, x, back in before:
            if self.active(STAGE_OF[u], back):
                return u, x, self.it - back + 3 - STAGE_OF[u]
        return user, -1, 0


def conv_seq_kernel(nc, ins, out):
    ctx = ExitStack()
    with ctx:
        def sb(name, shape, dt=F32):
            return ctx.enter_context(nc.sbuf_tensor(name, shape, dt))

        def count(name, per_image, unit=1):
            return Count(ctx.enter_context(nc.semaphore(name)), per_image, unit)

        const = sb("const", [128, CONST_W])
        ident, group_avg = const[:, 0:128], const[:, 128 + WIN:CONST_W]
        ident_r = sb("ident_r", [128, 128], F32R)
        mask_r = sb("mask_r", [128, WIN], F32R)
        minus_half = sb("minus_half", [128, 1])
        wperc = sb("wperc", [128, 3 * TAPS])
        cols = sb("cols", [128, 24])
        b_perc, b_up1, b_up2, b_qkv = cols[:, 0:3], cols[:, 3:5], cols[:, 5:6], cols[:, 6:9]
        gamma, beta, bq1, bk1, bv1, bp1 = (cols[:, 9 + k:10 + k] for k in range(6))
        b_hid, bq0_s, bq1_s, b_tot = cols[:, 15:17], cols[:, 17:18], cols[:, 18:19], cols[:, 19:20]
        bv0_row = sb("bv0_row", [128, 128])
        wc_hi, wc_lo = (sb(f"wc_{p}", [128, TAPS, D], F32R) for p in ("hi", "lo"))
        w2_hi, w2_lo = (sb(f"w2_{p}", [128, 2, 128], F32R) for p in ("hi", "lo"))
        w0_hi, w0_lo = (sb(f"w0_{p}", [128, 3, 128], F32R) for p in ("hi", "lo"))
        w1_hi, w1_lo = (sb(f"w1_{p}", [128, 3, 128], F32R) for p in ("hi", "lo"))

        x_in = sb("x_in", [128, TILES, 128])
        x_t = sb("x_t", [128, PIX])
        xp_hi, xp_lo = (sb(f"xp_{p}", [128, HP, WP], F32R) for p in ("hi", "lo"))
        g = sb("g", [128, 2, HALF])
        g_hi, g_lo = (sb(f"g_{p}", [128, 2, HALF], F32R) for p in ("hi", "lo"))
        h = sb("h", [128, PIX])
        h_hi, h_lo = (sb(f"h_{p}", [128, PIX], F32R) for p in ("hi", "lo"))
        q_hi, q_lo = (sb(f"q_{p}", [128, PIX], F32R) for p in ("hi", "lo"))
        kp_hi, kp_lo = (sb(f"kp_{p}", [128, HP, WP], F32R) for p in ("hi", "lo"))
        v_full = sb("v_full", [128, 4, 128])
        v_hl = sb("v_hl", [128, TILES, 2, 128], F32R)
        v_halo = sb("v_halo", [64, TILES, 2, 128], F32R)

        nm0 = sb("nm0", [128, TILES])
        sum0 = sb("sum0", [128, TILES])
        rec0 = sb("rec0", [128, TILES])
        p0 = sb("p0", [128, 4, 6, WP])
        pn = sb("pn", [128, 2, 6, W])
        pt_hi, pt_lo = (sb(f"pt_{p}", [128, 4, 128], F32R) for p in ("hi", "lo"))
        y = sb("y", [128, PIX])
        stats = sb("stats", [128, 4, 6])
        moments = sb("moments", [128, 2])
        g_mom = sb("g_mom", [128, 2])
        gn = sb("gn", [128, 5])
        neg_var, var_eps, rstd, gn_a, gn_nb = (gn[:, k:k + 1] for k in range(5))
        xn_hi, xn_lo = (sb(f"xn_{p}", [128, PIX], F32R) for p in ("hi", "lo"))

        qq_hi, qq_lo = (sb(f"qq_{p}", [128, PIX], F32R) for p in ("hi", "lo"))
        kk_hi, kk_lo = (sb(f"kk_{p}", [128, PIX], F32R) for p in ("hi", "lo"))
        vv_hi, vv_lo = (sb(f"vv_{p}", [128, TILES, 128], F32R) for p in ("hi", "lo"))
        nm1 = sb("nm1", [128, TILES])
        sum1 = sb("sum1", [128, TILES])
        rec1 = sb("rec1", [128, TILES])
        e = sb("e", [128, PIX])
        et_hi, et_lo = (sb(f"et_{p}", [128, TILES, HALF], F32R) for p in ("hi", "lo"))
        r_tok = sb("r_tok", [128, TILES, 128])
        a_t = sb("a_t", [128, HALF])
        o_sb = sb("o_sb", [128, TILES, 128])

        ps_s = ctx.enter_context(nc.psum_tensor("ps_s", [128, PIX], F32))
        ps_t = ctx.enter_context(nc.psum_tensor("ps_t", [128, PIX], F32))
        work = [ctx.enter_context(nc.psum_tensor(f"work{k}", [128, HALF], F32)) for k in range(4)]

        def bank(user, idx):
            return work[BANK_OF[user, idx]]

        x_loaded = count("x_loaded", 1, 16)
        halo_loaded = count("halo_loaded", 2, 16)
        stored = [count(f"stored{k}", 1, 16) for k in range(2)]
        pe = {u: count(f"pe_{u}", k) for u, k in dict(
            xt=2, conv=4, up2=2, q=2, k=2, v=2, av=4, at=4, gn=1, qq=2, kk=2, vv=2, xbt=2, pv=2,
            ft=2, s=8, t=8).items()}
        pe["as"] = count("pe_as", 4)
        x_t_ready, xp_hi_ready, xp_lo_ready = count("x_t_ready", 2), count("xp_hi_ready", 2), count("xp_lo_ready", 2)
        g_ready, g_hi_ready, g_lo_ready = count("g_ready", 4), count("g_hi_ready", 4), count("g_lo_ready", 4)
        h_ready, h_hi_ready, h_lo_ready = count("h_ready", 2), count("h_hi_ready", 2), count("h_lo_ready", 2)
        q_hi_ready, q_lo_ready = count("q_hi_ready", 2), count("q_lo_ready", 2)
        k_hi_ready, k_lo_ready = count("k_hi_ready", 2), count("k_lo_ready", 2)
        v_ready, v_hi_ready, v_lo_ready = count("v_ready", 2), count("v_hi_ready", 2), count("v_lo_ready", 2)
        max0_ready, p0_ready, rec0_ready, p0n_ready = (
            count("max0_ready", 4), count("p0_ready", 4), count("rec0_ready", 4), count("p0n_ready", 4))
        pt_hi_ready, pt_lo_ready = count("pt_hi_ready", 4), count("pt_lo_ready", 4)
        y_ready, stat_ready = count("y_ready", 4), count("stat_ready", 4)
        gn_step = count("gn_step", 7)
        rstd_ready = count("rstd_ready", 1)
        xn_ready, xn_hi_ready, xn_lo_ready, xb_ready = (
            count("xn_ready", 2), count("xn_hi_ready", 2), count("xn_lo_ready", 2), count("xb_ready", 2))
        qq_hi_ready, qq_lo_ready = count("qq_hi_ready", 2), count("qq_lo_ready", 2)
        kk_hi_ready, kk_lo_ready = count("kk_hi_ready", 2), count("kk_lo_ready", 2)
        vv_hi_ready, vv_lo_ready = count("vv_hi_ready", 2), count("vv_lo_ready", 2)
        r_tok_ready = count("r_tok_ready", 2)
        max1_ready, e_ready, et_hi_ready, et_lo_ready = (
            count("max1_ready", 8), count("e_ready", 8), count("et_hi_ready", 8), count("et_lo_ready", 8))
        a_t_ready, rec1_ready, o_ready = count("a_t_ready", 2), count("rec1_ready", 2), count("o_ready", 2)
        loads = ctx.enter_context(nc.semaphore("loads"))
        set_pe = ctx.enter_context(nc.semaphore("set_pe"))
        set_dve = ctx.enter_context(nc.semaphore("set_dve"))
        set_act = ctx.enter_context(nc.semaphore("set_act"))
        set_pool = ctx.enter_context(nc.semaphore("set_pool"))

        FREED_BY = dict(xt=x_t_ready, conv=g_ready, up2=h_ready, q=q_lo_ready, k=k_lo_ready, v=v_ready,
                        at=pt_lo_ready, av=y_ready, gn=gn_step, qq=qq_lo_ready, kk=kk_lo_ready,
                        vv=vv_lo_ready, xbt=r_tok_ready, pv=a_t_ready, ft=o_ready)
        FREED_BY["as"] = p0_ready

        def bank_free(turn, user, idx):
            u, x, n = turn.previous_user(user, idx)
            return FREED_BY[u].after(n, 2 if (u, x) == ("gn", 0) else x)

        x_view = ins["x"].rearrange("b (t r) w c -> (r w) (b t) c", r=4)
        out_view = out.rearrange("b (t r) w c -> (r w) (b t) c", r=4)

        w_up1 = e[:, 0:768].rearrange("p (m f) -> p m f", m=2)
        w_up1_t = g[:, :, :].rearrange("p m f -> p (m f)")[:, 0:768].rearrange("p (j d) -> p j d", j=3)
        wc_f = h[:, :].rearrange("p (s d) -> p s d", s=4)
        w_up2 = y[:, 0:256]
        w_qkv = y[:, 256:640].rearrange("p (m c) -> p m c", m=3)
        wv_t, wvp = y[:, 640:768], y[:, 768:896]
        wl1 = r_tok[:, 0:4, :]

        block = ctx.enter_context(nc.Block())
        N_LOADS = 11

        def run_turns(eng, turn_program):
            for it in (-2, -1, 0):
                turn_program(Turn(it))
            with eng.Fori(1, B - 2) as i:
                turn_program(Turn(i))
            for it in (B - 2, B - 1):
                turn_program(Turn(it))

        @block.sync
        def _(sp):
            def load(dst, src):
                sp.dma_start(dst, src).then_inc(loads, 16)

            sp.dma_start(x_in[:, :, :], x_view[:, 0:TILES, :]).then_inc(x_loaded.handle, 16)
            load(const[:, :], ins["const"])
            load(w_up1, ins["L0_conv_w_up1"].rearrange("(m p) f a b -> p m (f a b)", m=2))
            load(wperc[:, :], ins["L0_conv_w_perc"].rearrange("(c j) a y x -> c (j a y x)", j=3))
            load(cols[:, 0:15], ins["cols"])
            load(w_up2, ins["L0_conv_w_up2"].rearrange("p f a b -> p (f a b)"))
            load(w_qkv, ins["L0_conv_w_qkv"].rearrange("(m p) c -> p m c", m=3))
            load(bv0_row[:, :], ins["L0_conv_b_qkv"][2 * C:3 * C].rearrange("(a c) -> a c", a=1)
                 .broadcast_to([128, 128]))
            for k, name in enumerate(("Wq", "Wk", "Wv", "Wp")):
                load(wl1[:, k, :], ins[f"L1_conv_{name}"])

            def turn_program(turn):
                a, c = turn.a, turn.c
                if turn.active(1) and turn.active(1, back=-1):
                    sp.wait_ge(*x_t_ready.after(c, 1))
                    sp.dma_start(x_in[:, :, :], x_view[:, bass.ds((c + 1) * TILES, TILES), :]) \
                      .then_inc(x_loaded.handle, 16)
                if turn.active(3):
                    sp.wait_ge(*o_ready.after(a, 0))
                    sp.dma_start(out_view[:, bass.ds(a * TILES, 4), :], o_sb[:, 0:4, :]) \
                      .then_inc(stored[0].handle, 16)
                if turn.active(1):
                    sp.wait_ge(*v_lo_ready.after(c, 1))
                    sp.dma_start(v_halo[0:32, 0:TILES - 1].bitcast(F32), v_hl[0:32, 1:TILES].bitcast(F32)) \
                      .then_inc(halo_loaded.handle, 16)
                    sp.dma_start(v_halo[32:64, 1:TILES].bitcast(F32), v_hl[96:128, 0:TILES - 1].bitcast(F32)) \
                      .then_inc(halo_loaded.handle, 16)
                if turn.active(3):
                    sp.wait_ge(*o_ready.after(a, 1))
                    sp.dma_start(out_view[:, bass.ds(a * TILES + 4, 4), :], o_sb[:, 4:8, :]) \
                      .then_inc(stored[1].handle, 16)

            for it in (-2, -1, 0):
                turn_program(Turn(it))
            with sp.Fori(1, B - 3) as i:
                turn_program(Turn(i))
            for it in (B - 3, B - 2, B - 1):
                turn_program(Turn(it))
            for s in stored:
                sp.wait_ge(*s.after(B - 1, 0))

        @block.tensor
        def _(te):
            def mm3(dst, w_pair, x_pair, first=True, last=True):
                (wh, wl), (xh, xl) = w_pair, x_pair
                te.matmul(dst, wh, xl, start=first, stop=False)
                te.matmul(dst, wl, xh, start=False, stop=False)
                return te.matmul(dst, wh, xh, start=False, stop=last)

            def xt(turn, k):
                n = turn.c
                te.wait_ge(*x_loaded.after(n, 0))
                te.wait_ge(*bank_free(turn, "xt", k))
                for t in range(4):
                    mm = te.transpose(bank("xt", k)[:, t * 128:(t + 1) * 128], x_in[:, 4 * k + t, :], ident)
                mm.then_inc(pe["xt"].handle, 1)

            def conv(turn, k):
                n, half, m = turn.c, k // 2, k % 2
                te.wait_ge(*xp_lo_ready.after(n, 1))
                te.wait_ge(*bank_free(turn, "conv", k))
                dst = bank("conv", k)[:, :].rearrange("p (r w) -> p r w", r=ROWS)
                for tap in range(TAPS):
                    r0, c0 = half * ROWS + tap // 3, tap % 3
                    xs = [xp[:, r0:r0 + ROWS, c0:c0 + W] for xp in (xp_hi, xp_lo)]
                    ws = [wc[:, tap, m * 128:(m + 1) * 128] for wc in (wc_hi, wc_lo)]
                    mm = mm3(dst, ws, xs, tap == 0, tap == TAPS - 1)
                mm.then_inc(pe["conv"].handle, 1)

            def up2(turn, half):
                n = turn.c
                te.wait_ge(*g_lo_ready.after(n, 2 * half + 1))
                te.wait_ge(*bank_free(turn, "up2", half))
                for m in range(2):
                    mm = mm3(bank("up2", half)[:, :], (w2_hi[:, m, :], w2_lo[:, m, :]),
                             (g_hi[:, m, :], g_lo[:, m, :]), m == 0, m == 1)
                mm.then_inc(pe["up2"].handle, 1)

            def project(turn, user, half, n, ready, w_pair, x_pair):
                te.wait_ge(*ready.after(n, half))
                te.wait_ge(*bank_free(turn, user, half))
                cols_ = slice(half * HALF, (half + 1) * HALF)
                mm3(bank(user, half)[:, :], w_pair, [x[:, cols_] for x in x_pair]) \
                    .then_inc(pe[user].handle, 1)

            def project_pixels(turn, user, half, n, ready, w_pair, x_pair):
                te.wait_ge(*ready.after(n, half))
                te.wait_ge(*bank_free(turn, user, half))
                for t in range(4):
                    pix = slice((4 * half + t) * 128, (4 * half + t + 1) * 128)
                    mm = mm3(bank(user, half)[:, t * 128:(t + 1) * 128], [x[:, pix] for x in x_pair], w_pair)
                mm.then_inc(pe[user].handle, 1)

            def q(turn, half):
                project(turn, "q", half, turn.c, h_lo_ready, (w0_hi[:, 0], w0_lo[:, 0]), (h_hi, h_lo))

            def k(turn, half):
                project(turn, "k", half, turn.c, h_lo_ready, (w0_hi[:, 1], w0_lo[:, 1]), (h_hi, h_lo))

            def v(turn, half):
                project_pixels(turn, "v", half, turn.c, h_lo_ready, (w0_hi[:, 2], w0_lo[:, 2]), (h_hi, h_lo))

            def local_scores(turn, j):
                n = turn.b
                te.wait_ge(*q_lo_ready.after(n, j // 2))
                te.wait_ge(*k_lo_ready.after(n, 1))
                te.wait_ge(*bank_free(turn, "as", j))
                for u in range(2):
                    t = 2 * j + u
                    dst = bank("as", j)[:, u * WIN:(u + 1) * WIN]
                    qs = [x[:, t * 128:(t + 1) * 128] for x in (q_hi, q_lo)]
                    ks = [x[:, 4 * t:4 * t + 6, :].rearrange("p r w -> p (r w)") for x in (kp_hi, kp_lo)]
                    mm3(dst, qs, ks, True, False)
                    mm = te.matmul(dst, ident_r[:, :], mask_r[:, :], start=False, stop=True)
                mm.then_inc(pe["as"].handle, 1)

            def local_probs_t(turn, j):
                n = turn.b
                te.wait_ge(*p0n_ready.after(n, j))
                te.wait_ge(*bank_free(turn, "at", j))
                for u in range(2):
                    p = pn[:, u, 0:4, :].rearrange("p r w -> p (r w)")
                    te.transpose(bank("at", j)[:, u * 128:(u + 1) * 128], p, ident)
                for u in range(2):
                    p = pn[:, u, 4:6, :].rearrange("p r w -> p (r w)")
                    mm = te.transpose(bank("at", j)[0:64, (2 + u) * 128:(3 + u) * 128], p, ident)
                mm.then_inc(pe["at"].handle, 1)

            def local_values(turn, j):
                n = turn.b
                te.wait_ge(*pt_lo_ready.after(n, j))
                te.wait_ge(*halo_loaded.after(n, 1))
                te.wait_ge(*bank_free(turn, "av", j))
                for u in range(2):
                    t = 2 * j + u
                    dst = bank("av", j)[:, u * 128:(u + 1) * 128]
                    mm3(dst, (v_hl[:, t, 0, :], v_hl[:, t, 1, :]), (pt_hi[:, u, :], pt_lo[:, u, :]), True, False)
                    mm = mm3(dst, (v_halo[:, t, 0, :], v_halo[:, t, 1, :]),
                             (pt_hi[0:64, 2 + u, :], pt_lo[0:64, 2 + u, :]), False, True)
                mm.then_inc(pe["av"].handle, 1)

            def group_moments(turn):
                n = turn.b
                te.wait_ge(*gn_step.after(n, 1))
                te.wait_ge(*bank_free(turn, "gn", 0))
                te.matmul(bank("gn", 0)[:, 0:2], group_avg, moments[:, :], start=True, stop=True) \
                  .then_inc(pe["gn"].handle, 1)

            def qq(turn, half):
                project(turn, "qq", half, turn.b, xn_lo_ready, (w1_hi[:, 0], w1_lo[:, 0]), (xn_hi, xn_lo))

            def kk(turn, half):
                project(turn, "kk", half, turn.b, xn_lo_ready, (w1_hi[:, 1], w1_lo[:, 1]), (xn_hi, xn_lo))

            def vv(turn, half):
                project_pixels(turn, "vv", half, turn.b, xn_lo_ready, (w1_hi[:, 2], w1_lo[:, 2]), (xn_hi, xn_lo))

            def residual_t(turn, half):
                n = turn.a
                te.wait_ge(*xb_ready.after(n, half))
                te.wait_ge(*bank_free(turn, "xbt", half))
                for t in range(4):
                    pix = slice((4 * half + t) * 128, (4 * half + t + 1) * 128)
                    mm = te.transpose(bank("xbt", half)[:, t * 128:(t + 1) * 128], y[:, pix], ident)
                mm.then_inc(pe["xbt"].handle, 1)

            def scores(n, t):
                te.wait_ge(*qq_lo_ready.after(n, t // 4))
                te.wait_ge(*kk_lo_ready.after(n, 1))
                te.wait_ge(*e_ready.after(n, t - 1))
                for half in range(2):
                    keys = slice(half * HALF, (half + 1) * HALF)
                    mm = mm3(ps_s[:, keys], [x[:, t * 128:(t + 1) * 128] for x in (qq_hi, qq_lo)],
                             [x[:, keys] for x in (kk_hi, kk_lo)])
                mm.then_inc(pe["s"].handle, 1)

            def probs_t(n, t):
                te.wait_ge(*e_ready.after(n, t))
                te.wait_ge(*et_lo_ready.after(n, t - 1))
                for kt in range(TILES):
                    mm = te.transpose(ps_t[:, kt * 128:(kt + 1) * 128], e[:, kt * 128:(kt + 1) * 128], ident)
                mm.then_inc(pe["t"].handle, 1)

            def values(turn, half):
                n = turn.a
                te.wait_ge(*et_lo_ready.after(n, 4 * half + 3))
                te.wait_ge(*vv_lo_ready.after(n, 1))
                te.wait_ge(*bank_free(turn, "pv", half))
                for kt in range(TILES):
                    mm = mm3(bank("pv", half)[:, :], (vv_hi[:, kt, :], vv_lo[:, kt, :]),
                             (et_hi[:, kt, :], et_lo[:, kt, :]), kt == 0, kt == TILES - 1)
                mm.then_inc(pe["pv"].handle, 1)

            def final_t(turn, half):
                n = turn.a
                te.wait_ge(*a_t_ready.after(n, half))
                te.wait_ge(*bank_free(turn, "ft", half))
                for t in range(4):
                    mm = te.transpose(bank("ft", half)[:, t * 128:(t + 1) * 128], a_t[:, t * 128:(t + 1) * 128], ident)
                mm.then_inc(pe["ft"].handle, 1)

            te.wait_ge(loads, 16 * N_LOADS)
            for j in range(3):
                for m in range(2):
                    dst = ps_s[:, (2 * j + m) * 128:(2 * j + m + 1) * 128]
                    mm = te.transpose(dst, w_up1[:, m, j:3 * C:3], ident)
            mm.then_inc(set_pe, 1)
            for m in range(2):
                te.transpose(work[0][:, m * 128:(m + 1) * 128], w_up2[:, m * 128:(m + 1) * 128], ident)
            te.transpose(work[0][:, 256:384], wl1[:, 2, :], ident).then_inc(set_pe, 1)
            for m in range(3):
                mm = te.transpose(work[1][:, m * 128:(m + 1) * 128], w_qkv[:, m, :], ident)
            mm.then_inc(set_pe, 1)
            te.wait_ge(set_dve, 2)
            te.matmul(work[2][:, 0:128], wv_t, wl1[:, 3, :], start=True, stop=True)
            te.matmul(work[2][:, 128:129], wl1[:, 3, :], bv1, start=True, stop=True)
            for m in range(2):
                for j in range(3):
                    mm = te.matmul(work[2][:, 129 + m:130 + m], w_up1_t[:, j, m * 128:(m + 1) * 128],
                                   b_perc[:, j:j + 1], start=(j == 0), stop=(j == 2))
            mm.then_inc(set_pe, 1)
            te.wait_ge(set_dve, 4)
            te.wait_ge(set_act, 1)
            te.wait_ge(set_pool, 2)

            def turn_program(turn):
                p1, p2, p3 = turn.active(1), turn.active(2), turn.active(3)
                a, b = turn.a, turn.b
                if p1:
                    xt(turn, 0)
                    xt(turn, 1)
                if p3:
                    residual_t(turn, 0)
                    residual_t(turn, 1)
                if p2:
                    local_scores(turn, 0)
                if p3:
                    probs_t(a, 0)
                    scores(a, 1)
                if p1:
                    conv(turn, 0)
                if p3:
                    probs_t(a, 1)
                if p2:
                    local_probs_t(turn, 0)
                if p3:
                    scores(a, 2)
                if p2:
                    local_scores(turn, 1)
                if p1:
                    conv(turn, 1)
                if p3:
                    probs_t(a, 2)
                if p2:
                    local_values(turn, 0)
                    local_probs_t(turn, 1)
                if p3:
                    scores(a, 3)
                if p2:
                    local_scores(turn, 2)
                if p1:
                    conv(turn, 2)
                if p3:
                    probs_t(a, 3)
                if p2:
                    local_values(turn, 1)
                    local_probs_t(turn, 2)
                if p3:
                    scores(a, 4)
                if p2:
                    local_scores(turn, 3)
                if p1:
                    up2(turn, 0)
                if p3:
                    values(turn, 0)
                if p3:
                    probs_t(a, 4)
                if p2:
                    local_values(turn, 2)
                    local_probs_t(turn, 3)
                if p3:
                    scores(a, 5)
                    final_t(turn, 0)
                if p1:
                    conv(turn, 3)
                if p3:
                    probs_t(a, 5)
                if p2:
                    local_values(turn, 3)
                if p3:
                    scores(a, 6)
                if p1:
                    q(turn, 0)
                    k(turn, 0)
                    v(turn, 0)
                    up2(turn, 1)
                if p3:
                    probs_t(a, 6)
                    scores(a, 7)
                if p2:
                    group_moments(turn)
                if p3:
                    probs_t(a, 7)
                if p1:
                    q(turn, 1)
                    k(turn, 1)
                    v(turn, 1)
                if p3:
                    values(turn, 1)
                if p2:
                    qq(turn, 0)
                    qq(turn, 1)
                    kk(turn, 0)
                    kk(turn, 1)
                if p3:
                    final_t(turn, 1)
                if p2:
                    vv(turn, 0)
                    vv(turn, 1)
                    scores(b, 0)

            run_turns(te, turn_program)

        @block.scalar
        def _(act):
            def xp_hi_half(n, k):
                act.wait_ge(*x_t_ready.after(n, k))
                act.wait_ge(*pe["conv"].after(n - 1, 3))
                dst = xp_hi[:, 1 + k * ROWS:1 + (k + 1) * ROWS, 1:1 + W]
                act.activation(dst, x_t[:, k * HALF:(k + 1) * HALF].rearrange("p (r w) -> p r w", r=ROWS),
                               ACT.Copy).then_inc(xp_hi_ready.handle, 1)

            def gelu(n, k):
                m = k % 2
                act.wait_ge(*pe["conv"].after(n, k))
                act.wait_ge(*g_lo_ready.after(n, k - 2))
                act.activation(g[:, m, :], bank("conv", k)[:, :], ACT.Gelu, bias=b_hid[:, m:m + 1]) \
                   .then_inc(g_ready.handle, 1)

            def h_hi_half(n, k):
                cols_ = slice(k * HALF, (k + 1) * HALF)
                act.wait_ge(*h_ready.after(n, k))
                act.wait_ge(*pe["v"].after(n - 1, 1))
                act.activation(h_hi[:, cols_], h[:, cols_], ACT.Copy).then_inc(h_hi_ready.handle, 1)

            def q_hi_half(n, k):
                act.wait_ge(*pe["q"].after(n, k))
                act.wait_ge(*pe["as"].after(n - 1, 3))
                act.activation(q_hi[:, k * HALF:(k + 1) * HALF], bank("q", k)[:, :], ACT.Identity, bias=bq0_s) \
                   .then_inc(q_hi_ready.handle, 1)

            def k_hi_half(n, k):
                act.wait_ge(*pe["k"].after(n, k))
                act.activation(kp_hi[:, 1 + k * ROWS:1 + (k + 1) * ROWS, 1:1 + W],
                               bank("k", k)[:, :].rearrange("p (r w) -> p r w", r=ROWS),
                               ACT.Identity, bias=b_qkv[:, 1:2]).then_inc(k_hi_ready.handle, 1)

            def v_hi_half(n, k):
                act.wait_ge(*v_ready.after(n, k))
                act.wait_ge(*pe["av"].after(n - 1, 3))
                act.activation(v_hl[:, 4 * k:4 * k + 4, 0, :], v_full[:, :, :], ACT.Copy) \
                   .then_inc(v_hi_ready.handle, 1)

            def local_exp(n, j):
                act.wait_ge(*max0_ready.after(n, j))
                act.wait_ge(*p0n_ready.after(n, j - 2))
                for u in range(2):
                    t = 2 * j + u
                    ins_ = act.activation(p0[:, 2 * (j % 2) + u], bank("as", j)[:, u * WIN:(u + 1) * WIN]
                                          .rearrange("p (r w) -> p r w", r=6), ACT.Exp,
                                          bias=nm0[:, t:t + 1], accum_out=sum0[:, t:t + 1])
                ins_.then_inc(p0_ready.handle, 1)

            def pt_hi_pair(n, j):
                src = bank("at", j)[:, :].rearrange("p (u c) -> p u c", u=4)
                act.wait_ge(*pe["at"].after(n, j))
                act.wait_ge(*pe["av"].after(n, j - 1))
                act.activation(pt_hi[:, 0:2], src[:, 0:2], ACT.Copy)
                act.activation(pt_hi[0:64, 2:4], src[0:64, 2:4], ACT.Copy).then_inc(pt_hi_ready.handle, 1)

            def xn_hi_half(n, k):
                cols_ = slice(k * HALF, (k + 1) * HALF)
                act.wait_ge(*xn_ready.after(n, k))
                act.wait_ge(*pe["vv"].after(n - 1, 1))
                act.activation(xn_hi[:, cols_], y[:, cols_], ACT.Copy).then_inc(xn_hi_ready.handle, 1)

            def qq_hi_half(n, k):
                act.wait_ge(*pe["qq"].after(n, k))
                act.wait_ge(*pe["s"].after(n - 1, 7))
                act.activation(qq_hi[:, k * HALF:(k + 1) * HALF], bank("qq", k)[:, :], ACT.Identity, bias=bq1_s) \
                   .then_inc(qq_hi_ready.handle, 1)

            def kk_hi_half(n, k):
                act.wait_ge(*pe["kk"].after(n, k))
                act.activation(kk_hi[:, k * HALF:(k + 1) * HALF], bank("kk", k)[:, :], ACT.Identity, bias=bk1) \
                   .then_inc(kk_hi_ready.handle, 1)

            def vv_hi_half(n, k):
                act.wait_ge(*pe["vv"].after(n, k))
                act.wait_ge(*pe["pv"].after(n - 1, 1))
                act.activation(vv_hi[:, 4 * k:4 * k + 4, :], bank("vv", k)[:, :].rearrange("p (t c) -> p t c", t=4),
                               ACT.Copy).then_inc(vv_hi_ready.handle, 1)

            def residual(n, k):
                act.wait_ge(*pe["xbt"].after(n, k))
                act.wait_ge(*o_ready.after(n - 1, k))
                act.activation(r_tok[:, 4 * k:4 * k + 4, :], bank("xbt", k)[:, :].rearrange("p (t c) -> p t c", t=4),
                               ACT.Copy).then_inc(r_tok_ready.handle, 1)

            def exp(n, t):
                act.wait_ge(*max1_ready.after(n, t))
                act.wait_ge(*pe["t"].after(n, t - 1))
                if t % 4 == 0:
                    act.wait_ge(*rec1_ready.after(n - 1, t // 4))
                act.activation(e[:, :], ps_s[:, :], ACT.Exp, bias=nm1[:, t:t + 1], accum_out=sum1[:, t:t + 1]) \
                   .then_inc(e_ready.handle, 1)

            def et_hi_tile(n, t):
                act.wait_ge(*pe["t"].after(n, t))
                if t % 4 == 0:
                    act.wait_ge(*pe["pv"].after(n, t // 4 - 1))
                act.activation(et_hi[:, :, (t % 4) * 128:(t % 4 + 1) * 128],
                               ps_t[:, :].rearrange("p (k c) -> p k c", k=TILES), ACT.Copy) \
                   .then_inc(et_hi_ready.handle, 1)

            def a_t_half(n, k):
                act.wait_ge(*pe["pv"].after(n, k))
                act.wait_ge(*pe["ft"].after(n, k - 1))
                act.activation(a_t[:, :], bank("pv", k)[:, :], ACT.Copy).then_inc(a_t_ready.handle, 1)

            act.wait_ge(loads, 16 * N_LOADS)
            act.activation(ident_r[:, :], ident, ACT.Copy)
            act.activation(mask_r[:, :], const[:, 128:128 + WIN], ACT.Copy)
            act.activation(bq0_s, b_qkv[:, 0:1], ACT.Copy, scale=SCALE)
            act.activation(bq1_s, bq1, ACT.Copy, scale=SCALE).then_inc(set_act, 1)
            act.wait_ge(set_act, 1)
            act.wait_ge(set_dve, 4)

            def turn_program(turn):
                p1, p2, p3 = turn.active(1), turn.active(2), turn.active(3)
                a, b, c = turn.a, turn.b, turn.c
                if p1:
                    xp_hi_half(c, 0)
                    xp_hi_half(c, 1)
                if p3:
                    residual(a, 0)
                    residual(a, 1)
                if p2:
                    local_exp(b, 0)
                if p3:
                    et_hi_tile(a, 0)
                    exp(a, 1)
                if p3:
                    et_hi_tile(a, 1)
                if p2:
                    pt_hi_pair(b, 0)
                if p3:
                    exp(a, 2)
                if p2:
                    local_exp(b, 1)
                if p3:
                    et_hi_tile(a, 2)
                if p1:
                    gelu(c, 0)
                    gelu(c, 1)
                if p2:
                    pt_hi_pair(b, 1)
                if p3:
                    exp(a, 3)
                if p2:
                    local_exp(b, 2)
                if p3:
                    et_hi_tile(a, 3)
                if p1:
                    gelu(c, 2)
                if p2:
                    pt_hi_pair(b, 2)
                if p3:
                    exp(a, 4)
                if p2:
                    local_exp(b, 3)
                if p1:
                    h_hi_half(c, 0)
                if p3:
                    et_hi_tile(a, 4)
                if p2:
                    pt_hi_pair(b, 3)
                if p3:
                    exp(a, 5)
                    a_t_half(a, 0)
                if p3:
                    et_hi_tile(a, 5)
                if p1:
                    gelu(c, 3)
                if p3:
                    exp(a, 6)
                if p1:
                    q_hi_half(c, 0)
                    k_hi_half(c, 0)
                    v_hi_half(c, 0)
                    h_hi_half(c, 1)
                if p3:
                    et_hi_tile(a, 6)
                    exp(a, 7)
                if p3:
                    et_hi_tile(a, 7)
                if p1:
                    q_hi_half(c, 1)
                    k_hi_half(c, 1)
                    v_hi_half(c, 1)
                if p2:
                    xn_hi_half(b, 0)
                    xn_hi_half(b, 1)
                if p3:
                    a_t_half(a, 1)
                if p2:
                    qq_hi_half(b, 0)
                    qq_hi_half(b, 1)
                    kk_hi_half(b, 0)
                    kk_hi_half(b, 1)
                    vv_hi_half(b, 0)
                    vv_hi_half(b, 1)
                    exp(b, 0)

            run_turns(act, turn_program)

        @block.gpsimd
        def _(pool):
            def minus(dst, full, hi):
                return pool.tensor_tensor(dst, full, hi, ALU.subtract)

            def xp_lo_half(n, k):
                inside = (slice(None), slice(1 + k * ROWS, 1 + (k + 1) * ROWS), slice(1, 1 + W))
                pool.wait_ge(*xp_hi_ready.after(n, k))
                minus(xp_lo[inside], x_t[:, k * HALF:(k + 1) * HALF].rearrange("p (r w) -> p r w", r=ROWS),
                      xp_hi[inside].bitcast(F32)).then_inc(xp_lo_ready.handle, 1)

            def g_lo_part(n, k):
                pool.wait_ge(*g_hi_ready.after(n, k))
                minus(g_lo[:, k % 2, :], g[:, k % 2, :], g_hi[:, k % 2, :].bitcast(F32)) \
                    .then_inc(g_lo_ready.handle, 1)

            def h_lo_half(n, k):
                cols_ = slice(k * HALF, (k + 1) * HALF)
                pool.wait_ge(*h_hi_ready.after(n, k))
                minus(h_lo[:, cols_], h[:, cols_], h_hi[:, cols_].bitcast(F32)).then_inc(h_lo_ready.handle, 1)

            def v_lo_half(n, k):
                pool.wait_ge(*v_hi_ready.after(n, k))
                minus(v_hl[:, 4 * k:4 * k + 4, 1, :], v_full[:, :, :], v_hl[:, 4 * k:4 * k + 4, 0, :].bitcast(F32)) \
                    .then_inc(v_lo_ready.handle, 1)

            def xn_lo_half(n, k):
                cols_ = slice(k * HALF, (k + 1) * HALF)
                pool.wait_ge(*xn_hi_ready.after(n, k))
                minus(xn_lo[:, cols_], y[:, cols_], xn_hi[:, cols_].bitcast(F32)).then_inc(xn_lo_ready.handle, 1)

            for t in (xp_hi, xp_lo, kp_hi, kp_lo):
                pool.memset(t[:, :, :].bitcast(F32), 0.0)
            pool.memset(v_halo[:, :, :, :].bitcast(F32), 0.0)
            pool.memset(minus_half[:, :], -0.5).then_inc(set_pool, 1)
            pool.wait_ge(set_pool, 1)
            pool.memset(sum0[:, :], 0.0).then_inc(set_pool, 1)

            def turn_program(turn):
                b, c = turn.b, turn.c
                if turn.active(1):
                    xp_lo_half(c, 0)
                    xp_lo_half(c, 1)
                    g_lo_part(c, 0)
                    g_lo_part(c, 1)
                    g_lo_part(c, 2)
                    h_lo_half(c, 0)
                    g_lo_part(c, 3)
                    v_lo_half(c, 0)
                    h_lo_half(c, 1)
                if turn.active(2):
                    pool.wait_ge(*gn_step.after(b, 4))
                    pool.tensor_tensor(rstd, var_eps, minus_half[:, :], ALU.pow).then_inc(rstd_ready.handle, 1)
                if turn.active(1):
                    v_lo_half(c, 1)
                if turn.active(2):
                    xn_lo_half(b, 0)
                    xn_lo_half(b, 1)

            run_turns(pool, turn_program)

        @block.vector
        def _(dve):
            def x_t_half(n, k):
                dve.wait_ge(*pe["xt"].after(n, k))
                dve.wait_ge(*xp_lo_ready.after(n - 1, k))
                dve.tensor_copy(x_t[:, k * HALF:(k + 1) * HALF], bank("xt", k)[:, :]).then_inc(x_t_ready.handle, 1)

            def g_hi_part(n, k):
                dve.wait_ge(*g_ready.after(n, k))
                dve.wait_ge(*pe["up2"].after(n, k // 2 - 1))
                dve.tensor_copy(g_hi[:, k % 2, :], g[:, k % 2, :]).then_inc(g_hi_ready.handle, 1)

            def h_half(n, k):
                cols_ = slice(k * HALF, (k + 1) * HALF)
                dve.wait_ge(*pe["up2"].after(n, k))
                dve.wait_ge(*h_lo_ready.after(n - 1, k))
                dve.scalar_tensor_tensor(h[:, cols_], bank("up2", k)[:, :], b_up2, x_t[:, cols_], ALU.add, ALU.add) \
                   .then_inc(h_ready.handle, 1)

            def biased_lo(dst, src, bias, hi):
                return dve.scalar_tensor_tensor(dst, src, bias, hi, ALU.add, ALU.subtract)

            def q_lo_half(n, k):
                cols_ = slice(k * HALF, (k + 1) * HALF)
                dve.wait_ge(*q_hi_ready.after(n, k))
                biased_lo(q_lo[:, cols_], bank("q", k)[:, :], bq0_s, q_hi[:, cols_].bitcast(F32)) \
                    .then_inc(q_lo_ready.handle, 1)

            def k_lo_half(n, k):
                inside = (slice(None), slice(1 + k * ROWS, 1 + (k + 1) * ROWS), slice(1, 1 + W))
                dve.wait_ge(*k_hi_ready.after(n, k))
                biased_lo(kp_lo[inside], bank("k", k)[:, :].rearrange("p (r w) -> p r w", r=ROWS),
                          b_qkv[:, 1:2], kp_hi[inside].bitcast(F32)).then_inc(k_lo_ready.handle, 1)

            def v_half(n, k):
                dve.wait_ge(*pe["v"].after(n, k))
                dve.wait_ge(*v_lo_ready.after(n, k - 1))
                dve.tensor_tensor(v_full[:, :, :], bank("v", k)[:, :].rearrange("p (t c) -> p t c", t=4),
                                  bv0_row[:, :].rearrange("p (a c) -> p a c", a=1).broadcast_to([128, 4, 128]),
                                  ALU.add).then_inc(v_ready.handle, 1)

            def local_max(n, j):
                dve.wait_ge(*pe["as"].after(n, j))
                dve.wait_ge(*p0_ready.after(n - 1, j))
                dve.tensor_reduce(nm0[:, 2 * j:2 * j + 2], bank("as", j)[:, 0:2 * WIN]
                                  .rearrange("p (u k) -> p u k", u=2), AX.X, ALU.max, negate=True) \
                   .then_inc(max0_ready.handle, 1)

            def local_norm(n, j):
                dve.wait_ge(*p0_ready.after(n, j))
                dve.reciprocal(rec0[:, 2 * j:2 * j + 2], sum0[:, 2 * j:2 * j + 2]).then_inc(rec0_ready.handle, 1)
                dve.wait_ge(*rec0_ready.after(n, j))
                dve.wait_ge(*pe["at"].after(n, j - 1))
                pair = p0[:, 2 * (j % 2):2 * (j % 2) + 2]
                for dst, src, rows in ((slice(0, 5), slice(1, 6), 5), (slice(5, 6), slice(0, 1), 1)):
                    rec = rec0[:, 2 * j:2 * j + 2].rearrange("p (u r w) -> p u r w", r=1, w=1)
                    ins_ = dve.tensor_tensor(pn[:, :, dst, :], pair[:, :, src, 1:1 + W],
                                             rec.broadcast_to([128, 2, rows, W]), ALU.mult)
                ins_.then_inc(p0n_ready.handle, 1)

            def pt_lo_pair(n, j):
                src = bank("at", j)[:, :].rearrange("p (u c) -> p u c", u=4)
                dve.wait_ge(*pt_hi_ready.after(n, j))
                dve.tensor_tensor(pt_lo[:, 0:2], src[:, 0:2], pt_hi[:, 0:2].bitcast(F32), ALU.subtract)
                dve.tensor_tensor(pt_lo[0:64, 2:4], src[0:64, 2:4], pt_hi[0:64, 2:4].bitcast(F32), ALU.subtract) \
                   .then_inc(pt_lo_ready.handle, 1)

            def y_pair(n, j):
                cols_ = slice(j * 256, (j + 1) * 256)
                dve.wait_ge(*pe["av"].after(n, j))
                dve.wait_ge(*pe["xbt"].after(n - 1, j // 2))
                dve.tensor_tensor(y[:, cols_], bank("av", j)[:, 0:256], h[:, cols_], ALU.add) \
                   .then_inc(y_ready.handle, 1)
                dve.wait_ge(*y_ready.after(n, j))
                dve.bn_stats(stats[:, j, :], y[:, cols_]).then_inc(stat_ready.handle, 1)

            def channel_moments(n):
                dve.bn_aggr(moments[:, :], stats[:, :, :].rearrange("p a s -> p (a s)")).then_inc(gn_step.handle, 1)
                dve.wait_ge(*gn_step.after(n, 0))
                dve.scalar_tensor_tensor(moments[:, 1:2], moments[:, 0:1], moments[:, 0:1], moments[:, 1:2],
                                         ALU.mult, ALU.add).then_inc(gn_step.handle, 1)

            def group_norm(n):
                dve.wait_ge(*pe["gn"].after(n, 0))
                dve.tensor_copy(g_mom[:, :], bank("gn", 0)[:, 0:2]).then_inc(gn_step.handle, 1)
                dve.wait_ge(*gn_step.after(n, 2))
                dve.scalar_tensor_tensor(neg_var, g_mom[:, 0:1], g_mom[:, 0:1], g_mom[:, 1:2],
                                         ALU.mult, ALU.subtract).then_inc(gn_step.handle, 1)
                dve.wait_ge(*gn_step.after(n, 3))
                dve.tensor_scalar(var_eps, neg_var, -1.0, EPS, ALU.mult, ALU.add).then_inc(gn_step.handle, 1)
                dve.wait_ge(*rstd_ready.after(n, 0))
                dve.tensor_tensor(gn_a, gamma, rstd, ALU.mult).then_inc(gn_step.handle, 1)
                dve.wait_ge(*gn_step.after(n, 5))
                dve.scalar_tensor_tensor(gn_nb, g_mom[:, 0:1], gn_a, beta, ALU.mult, ALU.subtract) \
                   .then_inc(gn_step.handle, 1)
                dve.wait_ge(*gn_step.after(n, 6))
                for k in range(2):
                    cols_ = slice(k * HALF, (k + 1) * HALF)
                    dve.tensor_scalar(y[:, cols_], y[:, cols_], gn_a, gn_nb, ALU.mult, ALU.subtract) \
                       .then_inc(xn_ready.handle, 1)

            def residual_bias(n, k):
                cols_ = slice(k * HALF, (k + 1) * HALF)
                dve.wait_ge(*xn_lo_ready.after(n, k))
                dve.tensor_scalar(y[:, cols_], y[:, cols_], b_tot, None, ALU.add).then_inc(xb_ready.handle, 1)

            def qq_lo_half(n, k):
                cols_ = slice(k * HALF, (k + 1) * HALF)
                dve.wait_ge(*qq_hi_ready.after(n, k))
                biased_lo(qq_lo[:, cols_], bank("qq", k)[:, :], bq1_s, qq_hi[:, cols_].bitcast(F32)) \
                    .then_inc(qq_lo_ready.handle, 1)

            def kk_lo_half(n, k):
                cols_ = slice(k * HALF, (k + 1) * HALF)
                dve.wait_ge(*kk_hi_ready.after(n, k))
                biased_lo(kk_lo[:, cols_], bank("kk", k)[:, :], bk1, kk_hi[:, cols_].bitcast(F32)) \
                    .then_inc(kk_lo_ready.handle, 1)

            def vv_lo_half(n, k):
                dve.wait_ge(*vv_hi_ready.after(n, k))
                dve.tensor_tensor(vv_lo[:, 4 * k:4 * k + 4, :], bank("vv", k)[:, :].rearrange("p (t c) -> p t c", t=4),
                                  vv_hi[:, 4 * k:4 * k + 4, :].bitcast(F32), ALU.subtract) \
                   .then_inc(vv_lo_ready.handle, 1)

            def row_max(n, t):
                dve.wait_ge(*pe["s"].after(n, t))
                dve.wait_ge(*e_ready.after(n - 1, t))
                dve.tensor_reduce(nm1[:, t:t + 1], ps_s[:, :], AX.X, ALU.max, negate=True) \
                   .then_inc(max1_ready.handle, 1)

            def et_lo_tile(n, t):
                cols_ = slice((t % 4) * 128, (t % 4 + 1) * 128)
                dve.wait_ge(*et_hi_ready.after(n, t))
                dve.tensor_tensor(et_lo[:, :, cols_], ps_t[:, :].rearrange("p (k c) -> p k c", k=TILES),
                                  et_hi[:, :, cols_].bitcast(F32), ALU.subtract).then_inc(et_lo_ready.handle, 1)

            def output(n, k):
                four = slice(4 * k, 4 * k + 4)
                dve.wait_ge(*e_ready.after(n, 4 * k + 3))
                dve.reciprocal(rec1[:, four], sum1[:, four]).then_inc(rec1_ready.handle, 1)
                dve.wait_ge(*rec1_ready.after(n, k))
                dve.wait_ge(*pe["ft"].after(n, k))
                dve.wait_ge(*r_tok_ready.after(n, k))
                dve.wait_ge(*stored[k].after(n - 1, 0))
                for t in range(4):
                    ins_ = dve.scalar_tensor_tensor(o_sb[:, 4 * k + t, :], bank("ft", k)[:, t * 128:(t + 1) * 128],
                                                    rec1[:, 4 * k + t:4 * k + t + 1], r_tok[:, 4 * k + t, :],
                                                    ALU.mult, ALU.add)
                ins_.then_inc(o_ready.handle, 1)

            own = ctx.enter_context(nc.semaphore("set_own"))
            done = [0]

            def step(ins_):
                ins_.then_inc(own, 1)
                done[0] += 1
                dve.wait_ge(own, done[0])

            def split(hi, lo, full):
                step(dve.tensor_copy(hi, full))
                dve.tensor_tensor(lo, full, hi.bitcast(F32), ALU.subtract)

            dve.wait_ge(loads, 16 * N_LOADS)
            dve.wait_ge(set_pe, 1)
            dve.tensor_copy(w_up1_t, ps_s[:, 0:768].rearrange("p (j d) -> p j d", j=3)).then_inc(set_dve, 1)
            dve.wait_ge(set_pe, 2)
            dve.tensor_copy(wv_t, work[0][:, 256:384]).then_inc(set_dve, 1)
            split(w2_hi[:, :, :], w2_lo[:, :, :], work[0][:, 0:256].rearrange("p (m c) -> p m c", m=2))
            dve.wait_ge(set_pe, 3)
            step(dve.tensor_copy(w_qkv, work[1][:, 0:384].rearrange("p (m c) -> p m c", m=3)))
            step(dve.tensor_scalar(w_qkv[:, 0, :], w_qkv[:, 0, :], SCALE, None, ALU.mult))
            split(w0_hi[:, :, :], w0_lo[:, :, :], w_qkv)
            step(dve.tensor_scalar(wl1[:, 0, :], wl1[:, 0, :], SCALE, None, ALU.mult))
            split(w1_hi[:, 0:2, :], w1_lo[:, 0:2, :], wl1[:, 0:2, :])
            dve.wait_ge(set_dve, 2)
            for tap in range(TAPS):
                acc = wc_f[:, tap % 4, :]
                step(dve.tensor_scalar(acc, w_up1_t[:, 0, :], wperc[:, tap:tap + 1], None, ALU.mult))
                for j in (1, 2):
                    col = j * TAPS + tap
                    step(dve.scalar_tensor_tensor(acc, w_up1_t[:, j, :], wperc[:, col:col + 1], acc,
                                                  ALU.mult, ALU.add))
                split(wc_hi[:, tap, :], wc_lo[:, tap, :], acc)
            dve.wait_ge(set_pe, 4)
            step(dve.tensor_copy(wvp, work[2][:, 0:128]))
            split(w1_hi[:, 2, :], w1_lo[:, 2, :], wvp)
            dve.tensor_tensor(b_tot, work[2][:, 128:129], bp1, ALU.add)
            dve.tensor_tensor(b_hid, work[2][:, 129:131], b_up1, ALU.add).then_inc(set_dve, 1)
            dve.wait_ge(set_dve, 3)
            dve.wait_ge(set_act, 1)
            dve.memset(neg_var, 0.0).then_inc(set_dve, 1)

            def turn_program(turn):
                p1, p2, p3 = turn.active(1), turn.active(2), turn.active(3)
                a, b, c = turn.a, turn.b, turn.c
                if p1:
                    x_t_half(c, 0)
                    x_t_half(c, 1)
                if p2:
                    local_max(b, 0)
                if p3:
                    et_lo_tile(a, 0)
                    row_max(a, 1)
                if p2:
                    local_norm(b, 0)
                if p3:
                    et_lo_tile(a, 1)
                    row_max(a, 2)
                if p2:
                    pt_lo_pair(b, 0)
                    local_max(b, 1)
                    local_norm(b, 1)
                if p3:
                    et_lo_tile(a, 2)
                if p2:
                    y_pair(b, 0)
                if p1:
                    g_hi_part(c, 0)
                    g_hi_part(c, 1)
                if p3:
                    row_max(a, 3)
                if p2:
                    pt_lo_pair(b, 1)
                    local_max(b, 2)
                    local_norm(b, 2)
                if p3:
                    et_lo_tile(a, 3)
                if p2:
                    y_pair(b, 1)
                if p1:
                    g_hi_part(c, 2)
                if p3:
                    row_max(a, 4)
                if p2:
                    pt_lo_pair(b, 2)
                    local_max(b, 3)
                    local_norm(b, 3)
                if p1:
                    h_half(c, 0)
                if p3:
                    et_lo_tile(a, 4)
                if p2:
                    y_pair(b, 2)
                if p3:
                    row_max(a, 5)
                if p2:
                    pt_lo_pair(b, 3)
                if p3:
                    output(a, 0)
                if p3:
                    et_lo_tile(a, 5)
                if p2:
                    y_pair(b, 3)
                    dve.wait_ge(*stat_ready.after(b, 3))
                if p3:
                    row_max(a, 6)
                if p2:
                    channel_moments(b)
                if p1:
                    g_hi_part(c, 3)
                    q_lo_half(c, 0)
                    k_lo_half(c, 0)
                    v_half(c, 0)
                    h_half(c, 1)
                if p3:
                    et_lo_tile(a, 6)
                    row_max(a, 7)
                if p2:
                    group_norm(b)
                if p3:
                    et_lo_tile(a, 7)
                if p1:
                    q_lo_half(c, 1)
                    k_lo_half(c, 1)
                    v_half(c, 1)
                if p2:
                    residual_bias(b, 0)
                    residual_bias(b, 1)
                    qq_lo_half(b, 0)
                    qq_lo_half(b, 1)
                    kk_lo_half(b, 0)
                    kk_lo_half(b, 1)
                if p3:
                    output(a, 1)
                if p2:
                    vv_lo_half(b, 0)
                    vv_lo_half(b, 1)
                    row_max(b, 0)

            run_turns(dve, turn_program)


_INS = ["x", "L0_conv_w_perc", "L0_conv_w_up1", "L0_conv_w_up2", "L0_conv_w_qkv", "L0_conv_b_qkv",
        "L1_conv_Wq", "L1_conv_Wk", "L1_conv_Wv", "L1_conv_Wp"]
_COLS = [("L0_conv_b_perc", 3), ("L0_conv_b_up1", 2), ("L0_conv_b_up2", 1), ("L0_conv_b_qkv", 3), ("L1_conv_gamma", 1),
         ("L1_conv_beta", 1), ("L1_conv_bq", 1), ("L1_conv_bk", 1), ("L1_conv_bv", 1), ("L1_conv_bp", 1)]


def kernel(**inputs):
    import numpy as np
    import concourse.bacc as bacc
    from concourse.bass_utils import run_bass_kernel_spmd

    const = np.zeros((128, CONST_W), np.float32)
    const[:, 0:128] = np.eye(128)
    row, col = np.arange(128) // W, np.arange(128) % W
    key_row, key_col = np.arange(WIN) // WP, np.arange(WIN) % WP
    dy, dx = key_row[None] - row[:, None], key_col[None] - col[:, None]
    const[:, 128:128 + WIN] = np.where((dy >= 0) & (dy <= 2) & (dx >= 0) & (dx <= 2), 0.0, MASKED)
    groups = np.arange(128) // GROUP
    const[:, 128 + WIN:] = (groups[:, None] == groups[None]) / GROUP

    nc = bacc.Bacc("TRN2", target_bir_lowering=False, num_devices=1)
    arrays, views = {}, {}
    cols = [np.asarray(inputs[name]).reshape(128, k) if name == "L0_conv_b_perc"
            else np.asarray(inputs[name]).reshape(k, 128).T for name, k in _COLS]
    extra = {"const": const, "cols": np.ascontiguousarray(np.concatenate(cols, axis=1))}
    for name in _INS + ["const", "cols"]:
        array = extra[name] if name in extra else np.ascontiguousarray(inputs[name])
        arrays[f"in_{name}"] = array
        views[name] = nc.dram_tensor(f"in_{name}", array.shape, mybir.dt.from_np(array.dtype), kind="ExternalInput").ap()
    out = nc.dram_tensor("out", (B, H, W, C), F32, kind="ExternalOutput").ap()
    conv_seq_kernel(nc, views, out)
    result = run_bass_kernel_spmd(nc, [arrays], core_ids=[0])
    return result.results[0]["out"]
```

```python
from contextlib import ExitStack

import concourse.bass as bass
from concourse import mybir

F32 = mybir.dt.float32
F32R = mybir.dt.float32r
ALU = mybir.AluOpType
ACT = mybir.ActivationFunctionType
AX = mybir.AxisListType

B, H, W, C = 16, 32, 32, 128
PIX = H * W
TILES = PIX // 128
HALF = PIX // 2
ROWS = H // 2
HP, WP = H + 2, W + 2
TAPS = 9
PAIRS = ROWS // 2
WINO = (1, 2, 0, 3)
WIN = 6 * WP
D = 2 * C
GROUP = C // 8
EPS = 1e-3
SCALE = float(C) ** -0.5
MASKED = -1e30
CONST_W = 128 + WIN + 128


class Count:

    def __init__(self, handle, per_image, unit=1):
        self.handle, self.per_image, self.unit = handle, per_image, unit

    def after(self, n, e):
        value = n * (self.per_image * self.unit) + (e + 1) * self.unit
        return self.handle, max(value, 0) if isinstance(value, int) else value


BANK_PLAN = [
    ("xbt", 0, 1), ("xbt", 1, 2), ("as", 0, 0), ("conv", 0, 1), ("conv", 1, 2), ("at", 0, 3),
    ("as", 1, 0), ("conv", 2, 1), ("conv", 3, 2), ("av", 0, 3), ("at", 1, 0), ("as", 2, 1),
    ("conv", 4, 2), ("conv", 5, 3), ("av", 1, 0), ("at", 2, 1), ("as", 3, 2), ("up2", 0, 3),
    ("conv", 6, 0), ("conv", 7, 1), ("av", 2, 3), ("at", 3, 2), ("av", 3, 0), ("q", 0, 1),
    ("k", 0, 3), ("v", 0, 2), ("gn", 0, 0), ("pv", 0, 1), ("up2", 1, 0), ("xt", 0, 2),
    ("xt", 1, 3), ("q", 1, 1), ("k", 1, 0), ("ft", 0, 2), ("v", 1, 3), ("qq", 0, 1),
    ("qq", 1, 0), ("kk", 0, 3), ("kk", 1, 2), ("vv", 0, 1), ("pv", 1, 0), ("ft", 1, 3),
    ("vv", 1, 2),
]
BANK_OF = {(u, e): bank for u, e, bank in BANK_PLAN}
STAGE_OF = dict(xt=0, conv=1, up2=1, q=1, k=1, v=1, av=2, at=2, gn=2, qq=2, kk=2, vv=2, xbt=3, pv=3, ft=3)
STAGE_OF["as"] = 2


class Turn:

    def __init__(self, it):
        self.it = it
        self.a, self.b, self.c, self.d = it, it + 1, it + 2, it + 3
        self.fixed = isinstance(it, int)

    def active(self, stage, back=0):
        if not self.fixed:
            return True
        return 0 <= self.it - back + 3 - stage < B

    def previous_user(self, user, e):
        at = [(u, x) for u, x, _ in BANK_PLAN].index((user, e))
        before = [(u, x, 0) for u, x, b in BANK_PLAN[:at] if b == BANK_OF[user, e]][::-1]
        whole = [(u, x) for u, x, b in BANK_PLAN if b == BANK_OF[user, e]][::-1]
        for back in range(1, 5):
            before += [(u, x, back) for u, x in whole]
        for u, x, back in before:
            if self.active(STAGE_OF[u], back):
                return u, x, self.it - back + 3 - STAGE_OF[u]
        return user, -1, 0


def conv_seq_kernel(nc, ins, out):
    ctx = ExitStack()
    with ctx:
        def sb(name, shape, dt=F32):
            return ctx.enter_context(nc.sbuf_tensor(name, shape, dt))

        def count(name, per_image, unit=1):
            return Count(ctx.enter_context(nc.semaphore(name)), per_image, unit)

        const = sb("const", [128, CONST_W])
        ident, group_avg = const[:, 0:128], const[:, 128 + WIN:CONST_W]
        ident_r = sb("ident_r", [128, 128], F32R)
        mask_r = sb("mask_r", [128, WIN], F32R)
        minus_half = sb("minus_half", [128, 1])
        wperc = sb("wperc", [128, 3, 3, 3])
        wperc_g = sb("wperc_g", [128, 3, 4, 3])
        cols = sb("cols", [128, 24])
        b_perc, b_up1, b_up2, b_qkv = cols[:, 0:3], cols[:, 3:5], cols[:, 5:6], cols[:, 6:9]
        gamma, beta, bq1, bk1, bv1, bp1 = (cols[:, 9 + k:10 + k] for k in range(6))
        b_hid, bq0_s, bq1_s, b_tot = cols[:, 15:17], cols[:, 17:18], cols[:, 18:19], cols[:, 19:20]
        bv0_row = sb("bv0_row", [128, 128])
        wc_hi, wc_lo = (sb(f"wc_{p}", [128, 4, 3, D], F32R) for p in ("hi", "lo"))
        w2_hi, w2_lo = (sb(f"w2_{p}", [128, 2, 128], F32R) for p in ("hi", "lo"))
        w0_hi, w0_lo = (sb(f"w0_{p}", [128, 3, 128], F32R) for p in ("hi", "lo"))
        w1_hi, w1_lo = (sb(f"w1_{p}", [128, 3, 128], F32R) for p in ("hi", "lo"))

        x_in = sb("x_in", [128, TILES, 128])
        xp = sb("xp", [128, HP, WP])
        t_f = sb("t_f", [128, 4, PAIRS, WP])
        t_hi, t_lo = (sb(f"t_{p}", [128, 4, PAIRS, WP], F32R) for p in ("hi", "lo"))
        u = sb("u", [128, 2, PAIRS, 2, W])
        g = sb("g", [128, 2, HALF])
        g_hi, g_lo = (sb(f"g_{p}", [128, 2, HALF], F32R) for p in ("hi", "lo"))
        h = sb("h", [128, PIX])
        h_hi, h_lo = (sb(f"h_{p}", [128, PIX], F32R) for p in ("hi", "lo"))
        q_hi, q_lo = (sb(f"q_{p}", [128, PIX], F32R) for p in ("hi", "lo"))
        kp_hi, kp_lo = (sb(f"kp_{p}", [128, HP, WP], F32R) for p in ("hi", "lo"))
        v_full = sb("v_full", [128, 4, 128])
        v_hl = sb("v_hl", [128, TILES, 2, 128], F32R)
        v_halo = sb("v_halo", [128, TILES // 2, 2, 128], F32R)

        nm0 = sb("nm0", [128, TILES])
        sum0 = sb("sum0", [128, TILES])
        rec0 = sb("rec0", [128, TILES])
        p0 = sb("p0", [128, 4, 6, WP])
        pn_own = sb("pn_own", [128, 2, 128])
        pn_halo = sb("pn_halo", [128, 384])
        pt_hi, pt_lo = (sb(f"pt_{p}", [128, 4, 128], F32R) for p in ("hi", "lo"))
        y = sb("y", [128, PIX])
        stats = sb("stats", [128, 4, 6])
        moments = sb("moments", [128, 2])
        g_mom = sb("g_mom", [128, 2])
        gn = sb("gn", [128, 5])
        neg_var, var_eps, rstd, gn_a, gn_nb = (gn[:, k:k + 1] for k in range(5))
        xn_hi, xn_lo = (sb(f"xn_{p}", [128, PIX], F32R) for p in ("hi", "lo"))

        qq_hi, qq_lo = (sb(f"qq_{p}", [128, PIX], F32R) for p in ("hi", "lo"))
        kk_hi, kk_lo = (sb(f"kk_{p}", [128, PIX], F32R) for p in ("hi", "lo"))
        vv_hi, vv_lo = (sb(f"vv_{p}", [128, TILES, 128], F32R) for p in ("hi", "lo"))
        nm1 = sb("nm1", [128, TILES])
        sum1 = sb("sum1", [128, TILES])
        rec1 = sb("rec1", [128, TILES])
        e = sb("e", [128, PIX])
        et_hi, et_lo = (sb(f"et_{p}", [128, TILES, HALF], F32R) for p in ("hi", "lo"))
        r_tok = sb("r_tok", [128, TILES, 128])
        a_t = sb("a_t", [128, HALF])
        o_sb = sb("o_sb", [128, 4, 128])

        ps_s = ctx.enter_context(nc.psum_tensor("ps_s", [128, PIX], F32))
        ps_t = ctx.enter_context(nc.psum_tensor("ps_t", [128, PIX], F32))
        work = [ctx.enter_context(nc.psum_tensor(f"work{k}", [128, HALF], F32)) for k in range(4)]

        def bank(user, idx):
            return work[BANK_OF[user, idx]]

        x_loaded = count("x_loaded", 1, 16)
        halo_loaded = count("halo_loaded", 4, 16)
        stored = count("stored", 2, 16)
        pe = {u: count(f"pe_{u}", k) for u, k in dict(
            xt=2, conv=8, up2=2, q=2, k=2, v=2, av=4, at=4, gn=1, qq=2, kk=2, vv=2, xbt=2, pv=2,
            ft=2, s=8, t=8).items()}
        pe["as"] = count("pe_as", 4)
        xp_ready, t_ready, t_hi_ready, t_lo_ready = (
            count("xp_ready", 2), count("t_ready", 2), count("t_hi_ready", 2), count("t_lo_ready", 2))
        u_step = count("u_step", 10)
        g_ready, g_hi_ready, g_lo_ready = count("g_ready", 4), count("g_hi_ready", 4), count("g_lo_ready", 4)
        h_ready, h_hi_ready, h_lo_ready = count("h_ready", 2), count("h_hi_ready", 2), count("h_lo_ready", 2)
        q_hi_ready, q_lo_ready = count("q_hi_ready", 2), count("q_lo_ready", 2)
        k_hi_ready, k_lo_ready = count("k_hi_ready", 2), count("k_lo_ready", 2)
        v_ready, v_hi_ready, v_lo_ready = count("v_ready", 2), count("v_hi_ready", 2), count("v_lo_ready", 2)
        max0_ready, p0_ready, rec0_ready, p0n_ready = (
            count("max0_ready", 4), count("p0_ready", 4), count("rec0_ready", 4), count("p0n_ready", 4))
        pt_hi_ready, pt_lo_ready = count("pt_hi_ready", 4), count("pt_lo_ready", 4)
        y_ready, stat_ready = count("y_ready", 4), count("stat_ready", 4)
        gn_step = count("gn_step", 7)
        rstd_ready = count("rstd_ready", 1)
        xn_ready, xn_hi_ready, xn_lo_ready, xb_ready = (
            count("xn_ready", 2), count("xn_hi_ready", 2), count("xn_lo_ready", 2), count("xb_ready", 2))
        qq_hi_ready, qq_lo_ready = count("qq_hi_ready", 2), count("qq_lo_ready", 2)
        kk_hi_ready, kk_lo_ready = count("kk_hi_ready", 2), count("kk_lo_ready", 2)
        vv_hi_ready, vv_lo_ready = count("vv_hi_ready", 2), count("vv_lo_ready", 2)
        r_tok_ready = count("r_tok_ready", 2)
        max1_ready, e_ready, et_hi_ready, et_lo_ready = (
            count("max1_ready", 8), count("e_ready", 8), count("et_hi_ready", 8), count("et_lo_ready", 8))
        a_t_ready, rec1_ready, o_ready = count("a_t_ready", 2), count("rec1_ready", 2), count("o_ready", 2)
        loads = ctx.enter_context(nc.semaphore("loads"))
        set_pe = ctx.enter_context(nc.semaphore("set_pe"))
        set_dve = ctx.enter_context(nc.semaphore("set_dve"))
        set_act = ctx.enter_context(nc.semaphore("set_act"))
        set_pool = ctx.enter_context(nc.semaphore("set_pool"))
        set_wc = ctx.enter_context(nc.semaphore("set_wc"))

        FREED_BY = dict(xt=xp_ready, conv=u_step, up2=h_ready, q=q_lo_ready, k=k_lo_ready, v=v_ready,
                        at=pt_lo_ready, av=y_ready, gn=gn_step, qq=qq_lo_ready, kk=kk_lo_ready,
                        vv=vv_lo_ready, xbt=r_tok_ready, pv=a_t_ready, ft=o_ready)
        FREED_BY["as"] = p0_ready

        def bank_free(turn, user, idx):
            u, x, n = turn.previous_user(user, idx)
            if x >= 0 and u == "gn":
                x = 2
            if x >= 0 and u == "conv":
                x = 5 * (x // 4) + (0, 2, 3, 4)[x % 4]
            return FREED_BY[u].after(n, x)

        def inside(padded, half):
            return padded[:, 1 + half * ROWS:1 + (half + 1) * ROWS, 1:1 + W]

        x_view = ins["x"].rearrange("b (t r) w c -> (r w) (b t) c", r=4)
        out_view = out.rearrange("b (t r) w c -> (r w) (b t) c", r=4)

        w_up1 = e[:, 0:768].rearrange("p (m f) -> p m f", m=2)
        w_up1_t = g[:, :, :].rearrange("p m f -> p (m f)")[:, 0:768].rearrange("p (j d) -> p j d", j=3)
        wc_f = h[:, :].rearrange("p (s d) -> p s d", s=4)
        w_up2 = y[:, 0:256]
        w_qkv = y[:, 256:640].rearrange("p (m c) -> p m c", m=3)
        wv_t, wvp = y[:, 640:768], y[:, 768:896]
        wl1 = r_tok[:, 0:4, :]

        block = ctx.enter_context(nc.Block())
        N_LOADS = 11

        def run_turns(eng, turn_program):
            for it in (-3, -2, -1, 0):
                turn_program(Turn(it))
            with eng.Fori(1, B - 3) as i:
                turn_program(Turn(i))
            for it in (B - 3, B - 2, B - 1):
                turn_program(Turn(it))

        @block.sync
        def _(sp):
            def load(dst, src):
                sp.dma_start(dst, src).then_inc(loads, 16)

            sp.dma_start(x_in[:, :, :], x_view[:, 0:TILES, :]).then_inc(x_loaded.handle, 16)
            load(const[:, :], ins["const"])
            load(w_up1, ins["L0_conv_w_up1"].rearrange("(m p) f a b -> p m (f a b)", m=2))
            load(wperc[:, :, :, :].rearrange("p j y x -> p (j y x)"),
                 ins["L0_conv_w_perc"].rearrange("(c j) a y x -> c (j a y x)", j=3))
            load(cols[:, 0:15], ins["cols"])
            load(w_up2, ins["L0_conv_w_up2"].rearrange("p f a b -> p (f a b)"))
            load(w_qkv, ins["L0_conv_w_qkv"].rearrange("(m p) c -> p m c", m=3))
            load(bv0_row[:, :], ins["L0_conv_b_qkv"][2 * C:3 * C].rearrange("(a c) -> a c", a=1)
                 .broadcast_to([128, 128]))
            for k, name in enumerate(("Wq", "Wk", "Wv", "Wp")):
                load(wl1[:, k, :], ins[f"L1_conv_{name}"])

            def turn_program(turn):
                a, c, d = turn.a, turn.c, turn.d
                if turn.active(3):
                    sp.wait_ge(*o_ready.after(a, 0))
                    sp.dma_start(out_view[:, bass.ds(a * TILES, 4), :], o_sb[:, :, :]).then_inc(stored.handle, 16)
                if turn.active(0) and turn.active(0, back=-1):
                    sp.wait_ge(*xp_ready.after(d, 1))
                    sp.dma_start(x_in[:, :, :], x_view[:, bass.ds((d + 1) * TILES, TILES), :]) \
                      .then_inc(x_loaded.handle, 16)
                if turn.active(1):
                    sp.wait_ge(*v_lo_ready.after(c, 1))
                    for dst, first, count_, src, tile in ((0, 1, 3, 96, 1), (64, 0, 4, 96, 0),
                                                          (32, 0, 4, 0, 1), (96, 0, 3, 0, 2)):
                        sp.dma_start(v_halo[dst:dst + 32, first:first + count_].bitcast(F32),
                                     v_hl[src:src + 32, tile:tile + 2 * count_ - 1:2].bitcast(F32)) \
                          .then_inc(halo_loaded.handle, 16)
                if turn.active(3):
                    sp.wait_ge(*o_ready.after(a, 1))
                    sp.dma_start(out_view[:, bass.ds(a * TILES + 4, 4), :], o_sb[:, :, :]).then_inc(stored.handle, 16)

            for it in (-3, -2, -1, 0):
                turn_program(Turn(it))
            with sp.Fori(1, B - 4) as i:
                turn_program(Turn(i))
            for it in (B - 4, B - 3, B - 2, B - 1):
                turn_program(Turn(it))
            sp.wait_ge(*stored.after(B - 1, 1))

        @block.tensor
        def _(te):
            def mm3(dst, w_pair, x_pair, first=True, last=True):
                (wh, wl), (xh, xl) = w_pair, x_pair
                te.matmul(dst, wh, xl, start=first, stop=False)
                te.matmul(dst, wl, xh, start=False, stop=False)
                return te.matmul(dst, wh, xh, start=False, stop=last)

            def xt(turn, k):
                n = turn.d
                te.wait_ge(*x_loaded.after(n, 0))
                te.wait_ge(*bank_free(turn, "xt", k))
                for t in range(4):
                    mm = te.transpose(bank("xt", k)[:, t * 128:(t + 1) * 128], x_in[:, 4 * k + t, :], ident)
                mm.then_inc(pe["xt"].handle, 1)

            def conv(turn, k):
                n, half, i = turn.c, k // 4, WINO[k % 4]
                te.wait_ge(*t_lo_ready.after(n, half))
                te.wait_ge(*bank_free(turn, "conv", k))
                for m in range(2):
                    dst = bank("conv", k)[:, m * 256:(m + 1) * 256].rearrange("p (r w) -> p r w", r=PAIRS)
                    for dx in range(3):
                        xs = [t[:, i, :, dx:dx + W] for t in (t_hi, t_lo)]
                        ws = [wc[:, i, dx, m * 128:(m + 1) * 128] for wc in (wc_hi, wc_lo)]
                        mm = mm3(dst, ws, xs, dx == 0, dx == 2)
                mm.then_inc(pe["conv"].handle, 1)

            def up2(turn, half):
                n = turn.c
                te.wait_ge(*g_lo_ready.after(n, 2 * half + 1))
                te.wait_ge(*bank_free(turn, "up2", half))
                for m in range(2):
                    mm = mm3(bank("up2", half)[:, :], (w2_hi[:, m, :], w2_lo[:, m, :]),
                             (g_hi[:, m, :], g_lo[:, m, :]), m == 0, m == 1)
                mm.then_inc(pe["up2"].handle, 1)

            def project(turn, user, half, n, ready, w_pair, x_pair):
                te.wait_ge(*ready.after(n, half))
                te.wait_ge(*bank_free(turn, user, half))
                cols_ = slice(half * HALF, (half + 1) * HALF)
                mm3(bank(user, half)[:, :], w_pair, [x[:, cols_] for x in x_pair]) \
                    .then_inc(pe[user].handle, 1)

            def project_pixels(turn, user, half, n, ready, w_pair, x_pair):
                te.wait_ge(*ready.after(n, half))
                te.wait_ge(*bank_free(turn, user, half))
                for t in range(4):
                    pix = slice((4 * half + t) * 128, (4 * half + t + 1) * 128)
                    mm = mm3(bank(user, half)[:, t * 128:(t + 1) * 128], [x[:, pix] for x in x_pair], w_pair)
                mm.then_inc(pe[user].handle, 1)

            def q(turn, half):
                project(turn, "q", half, turn.c, h_lo_ready, (w0_hi[:, 0], w0_lo[:, 0]), (h_hi, h_lo))

            def k(turn, half):
                project(turn, "k", half, turn.c, h_lo_ready, (w0_hi[:, 1], w0_lo[:, 1]), (h_hi, h_lo))

            def v(turn, half):
                project_pixels(turn, "v", half, turn.c, h_lo_ready, (w0_hi[:, 2], w0_lo[:, 2]), (h_hi, h_lo))

            def local_scores(turn, j):
                n = turn.b
                te.wait_ge(*q_lo_ready.after(n, j // 2))
                te.wait_ge(*k_lo_ready.after(n, 1))
                te.wait_ge(*bank_free(turn, "as", j))
                for u in range(2):
                    t = 2 * j + u
                    dst = bank("as", j)[:, u * WIN:(u + 1) * WIN]
                    qs = [x[:, t * 128:(t + 1) * 128] for x in (q_hi, q_lo)]
                    ks = [x[:, 4 * t:4 * t + 6, :].rearrange("p r w -> p (r w)") for x in (kp_hi, kp_lo)]
                    mm3(dst, qs, ks, True, False)
                    mm = te.matmul(dst, ident_r[:, :], mask_r[:, :], start=False, stop=True)
                mm.then_inc(pe["as"].handle, 1)

            def local_probs_t(turn, j):
                n = turn.b
                te.wait_ge(*p0n_ready.after(n, j))
                te.wait_ge(*bank_free(turn, "at", j))
                for u in range(2):
                    te.transpose(bank("at", j)[:, u * 128:(u + 1) * 128], pn_own[:, u, :], ident)
                for u in range(2):
                    mm = te.transpose(bank("at", j)[:, (2 + u) * 128:(3 + u) * 128],
                                      pn_halo[:, u * 128:(u + 1) * 128], ident)
                mm.then_inc(pe["at"].handle, 1)

            def local_values(turn, j):
                n = turn.b
                te.wait_ge(*pt_lo_ready.after(n, j))
                te.wait_ge(*halo_loaded.after(n, 3))
                te.wait_ge(*bank_free(turn, "av", j))
                mm3(bank("av", j)[:, 0:256], (v_halo[:, j, 0, :], v_halo[:, j, 1, :]),
                    [pt[:, 2:4, :].rearrange("p u c -> p (u c)") for pt in (pt_hi, pt_lo)], True, False)
                for u in range(2):
                    t = 2 * j + u
                    mm = mm3(bank("av", j)[:, u * 128:(u + 1) * 128], (v_hl[:, t, 0, :], v_hl[:, t, 1, :]),
                             (pt_hi[:, u, :], pt_lo[:, u, :]), False, u == 1)
                mm.then_inc(pe["av"].handle, 1)

            def group_moments(turn):
                n = turn.b
                te.wait_ge(*gn_step.after(n, 1))
                te.wait_ge(*bank_free(turn, "gn", 0))
                te.matmul(bank("gn", 0)[:, 0:2], group_avg, moments[:, :], start=True, stop=True) \
                  .then_inc(pe["gn"].handle, 1)

            def qq(turn, half):
                project(turn, "qq", half, turn.b, xn_lo_ready, (w1_hi[:, 0], w1_lo[:, 0]), (xn_hi, xn_lo))

            def kk(turn, half):
                project(turn, "kk", half, turn.b, xn_lo_ready, (w1_hi[:, 1], w1_lo[:, 1]), (xn_hi, xn_lo))

            def vv(turn, half):
                project_pixels(turn, "vv", half, turn.b, xn_lo_ready, (w1_hi[:, 2], w1_lo[:, 2]), (xn_hi, xn_lo))

            def residual_t(turn, half):
                n = turn.a
                te.wait_ge(*xb_ready.after(n, half))
                te.wait_ge(*bank_free(turn, "xbt", half))
                for t in range(4):
                    pix = slice((4 * half + t) * 128, (4 * half + t + 1) * 128)
                    mm = te.transpose(bank("xbt", half)[:, t * 128:(t + 1) * 128], y[:, pix], ident)
                mm.then_inc(pe["xbt"].handle, 1)

            def scores(n, t):
                te.wait_ge(*qq_lo_ready.after(n, t // 4))
                te.wait_ge(*kk_lo_ready.after(n, 1))
                te.wait_ge(*e_ready.after(n, t - 1))
                for half in range(2):
                    keys = slice(half * HALF, (half + 1) * HALF)
                    mm = mm3(ps_s[:, keys], [x[:, t * 128:(t + 1) * 128] for x in (qq_hi, qq_lo)],
                             [x[:, keys] for x in (kk_hi, kk_lo)])
                mm.then_inc(pe["s"].handle, 1)

            def probs_t(n, t):
                te.wait_ge(*e_ready.after(n, t))
                te.wait_ge(*et_lo_ready.after(n, t - 1))
                for kt in range(TILES):
                    mm = te.transpose(ps_t[:, kt * 128:(kt + 1) * 128], e[:, kt * 128:(kt + 1) * 128], ident)
                mm.then_inc(pe["t"].handle, 1)

            def values(turn, half):
                n = turn.a
                te.wait_ge(*et_lo_ready.after(n, 4 * half + 3))
                te.wait_ge(*vv_lo_ready.after(n, 1))
                te.wait_ge(*bank_free(turn, "pv", half))
                for kt in range(TILES):
                    mm = mm3(bank("pv", half)[:, :], (vv_hi[:, kt, :], vv_lo[:, kt, :]),
                             (et_hi[:, kt, :], et_lo[:, kt, :]), kt == 0, kt == TILES - 1)
                mm.then_inc(pe["pv"].handle, 1)

            def final_t(turn, half):
                n = turn.a
                te.wait_ge(*a_t_ready.after(n, half))
                te.wait_ge(*bank_free(turn, "ft", half))
                for t in range(4):
                    mm = te.transpose(bank("ft", half)[:, t * 128:(t + 1) * 128], a_t[:, t * 128:(t + 1) * 128], ident)
                mm.then_inc(pe["ft"].handle, 1)

            te.wait_ge(loads, 16 * N_LOADS)
            for j in range(3):
                for m in range(2):
                    dst = ps_s[:, (2 * j + m) * 128:(2 * j + m + 1) * 128]
                    mm = te.transpose(dst, w_up1[:, m, j:3 * C:3], ident)
            mm.then_inc(set_pe, 1)
            for m in range(2):
                te.transpose(work[0][:, m * 128:(m + 1) * 128], w_up2[:, m * 128:(m + 1) * 128], ident)
            te.transpose(work[0][:, 256:384], wl1[:, 2, :], ident).then_inc(set_pe, 1)
            for m in range(3):
                mm = te.transpose(work[1][:, m * 128:(m + 1) * 128], w_qkv[:, m, :], ident)
            mm.then_inc(set_pe, 1)
            te.wait_ge(set_dve, 2)
            te.matmul(work[2][:, 0:128], wv_t, wl1[:, 3, :], start=True, stop=True)
            te.matmul(work[2][:, 128:129], wl1[:, 3, :], bv1, start=True, stop=True)
            for m in range(2):
                for j in range(3):
                    mm = te.matmul(work[2][:, 129 + m:130 + m], w_up1_t[:, j, m * 128:(m + 1) * 128],
                                   b_perc[:, j:j + 1], start=(j == 0), stop=(j == 2))
            mm.then_inc(set_pe, 1)
            te.wait_ge(set_dve, 4)
            te.wait_ge(set_act, 13)
            te.wait_ge(set_pool, 13)

            def turn_program(turn):
                p0, p1, p2, p3 = (turn.active(k) for k in range(4))
                a, b = turn.a, turn.b
                if p3:
                    residual_t(turn, 0)
                    residual_t(turn, 1)
                if p2:
                    local_scores(turn, 0)
                if p3:
                    scores(a, 1)
                    probs_t(a, 0)
                if p1:
                    conv(turn, 0)
                    conv(turn, 1)
                if p3:
                    scores(a, 2)
                    probs_t(a, 1)
                if p2:
                    local_probs_t(turn, 0)
                    local_scores(turn, 1)
                if p1:
                    conv(turn, 2)
                    conv(turn, 3)
                if p2:
                    local_values(turn, 0)
                if p3:
                    scores(a, 3)
                    probs_t(a, 2)
                if p2:
                    local_probs_t(turn, 1)
                    local_scores(turn, 2)
                if p1:
                    conv(turn, 4)
                    conv(turn, 5)
                if p2:
                    local_values(turn, 1)
                if p3:
                    scores(a, 4)
                    probs_t(a, 3)
                if p2:
                    local_probs_t(turn, 2)
                    local_scores(turn, 3)
                if p1:
                    up2(turn, 0)
                    conv(turn, 6)
                    conv(turn, 7)
                if p2:
                    local_values(turn, 2)
                if p2:
                    local_probs_t(turn, 3)
                if p3:
                    scores(a, 5)
                    probs_t(a, 4)
                if p2:
                    local_values(turn, 3)
                if p1:
                    q(turn, 0)
                    k(turn, 0)
                    v(turn, 0)
                if p2:
                    group_moments(turn)
                if p3:
                    values(turn, 0)
                if p3:
                    scores(a, 6)
                if p1:
                    up2(turn, 1)
                if p3:
                    probs_t(a, 5)
                if p0:
                    xt(turn, 0)
                    xt(turn, 1)
                if p1:
                    q(turn, 1)
                    k(turn, 1)
                if p3:
                    scores(a, 7)
                    probs_t(a, 6)
                    final_t(turn, 0)
                if p1:
                    v(turn, 1)
                if p2:
                    qq(turn, 0)
                    qq(turn, 1)
                if p3:
                    probs_t(a, 7)
                if p2:
                    kk(turn, 0)
                    kk(turn, 1)
                    vv(turn, 0)
                if p3:
                    values(turn, 1)
                if p2:
                    scores(b, 0)
                if p3:
                    final_t(turn, 1)
                if p2:
                    vv(turn, 1)

            run_turns(te, turn_program)

        @block.scalar
        def _(act):
            def t_hi_half(n, k):
                act.wait_ge(*t_ready.after(n, k))
                act.wait_ge(*pe["conv"].after(n, 4 * k - 1))
                act.activation(t_hi[:, :, :, :], t_f[:, :, :, :], ACT.Copy).then_inc(t_hi_ready.handle, 1)

            def take_m1(n, half):
                act.wait_ge(*pe["conv"].after(n, 4 * half))
                act.wait_ge(*g_ready.after(n, 2 * half - 1))
                act.activation(u[:, :, :, 0, :], bank("conv", 4 * half)[:, :]
                               .rearrange("p (m r w) -> p m r w", m=2, r=PAIRS), ACT.Copy).then_inc(u_step.handle, 1)

            def gelu(n, k):
                m = k % 2
                act.wait_ge(*u_step.after(n, 5 * (k // 2) + 4))
                act.wait_ge(*g_lo_ready.after(n, k - 2))
                act.activation(g[:, m, :], u[:, m].rearrange("p r e w -> p (r e w)"), ACT.Gelu,
                               bias=b_hid[:, m:m + 1]).then_inc(g_ready.handle, 1)

            def h_hi_half(n, k):
                cols_ = slice(k * HALF, (k + 1) * HALF)
                act.wait_ge(*h_ready.after(n, k))
                act.wait_ge(*pe["v"].after(n - 1, 1))
                act.activation(h_hi[:, cols_], h[:, cols_], ACT.Copy).then_inc(h_hi_ready.handle, 1)

            def q_hi_half(n, k):
                act.wait_ge(*pe["q"].after(n, k))
                act.wait_ge(*pe["as"].after(n - 1, 3))
                act.activation(q_hi[:, k * HALF:(k + 1) * HALF], bank("q", k)[:, :], ACT.Identity, bias=bq0_s) \
                   .then_inc(q_hi_ready.handle, 1)

            def k_hi_half(n, k):
                act.wait_ge(*pe["k"].after(n, k))
                act.activation(kp_hi[:, 1 + k * ROWS:1 + (k + 1) * ROWS, 1:1 + W],
                               bank("k", k)[:, :].rearrange("p (r w) -> p r w", r=ROWS),
                               ACT.Identity, bias=b_qkv[:, 1:2]).then_inc(k_hi_ready.handle, 1)

            def v_hi_half(n, k):
                act.wait_ge(*v_ready.after(n, k))
                act.wait_ge(*pe["av"].after(n - 1, 3))
                act.activation(v_hl[:, 4 * k:4 * k + 4, 0, :], v_full[:, :, :], ACT.Copy) \
                   .then_inc(v_hi_ready.handle, 1)

            def local_exp(n, j):
                act.wait_ge(*max0_ready.after(n, j))
                act.wait_ge(*p0n_ready.after(n, j - 2))
                for u in range(2):
                    t = 2 * j + u
                    ins_ = act.activation(p0[:, 2 * (j % 2) + u], bank("as", j)[:, u * WIN:(u + 1) * WIN]
                                          .rearrange("p (r w) -> p r w", r=6), ACT.Exp,
                                          bias=nm0[:, t:t + 1], accum_out=sum0[:, t:t + 1])
                ins_.then_inc(p0_ready.handle, 1)

            def pt_hi_pair(n, j):
                act.wait_ge(*pe["at"].after(n, j))
                act.wait_ge(*pe["av"].after(n, j - 1))
                act.activation(pt_hi[:, :, :], bank("at", j)[:, :].rearrange("p (u c) -> p u c", u=4), ACT.Copy) \
                   .then_inc(pt_hi_ready.handle, 1)

            def xn_hi_half(n, k):
                cols_ = slice(k * HALF, (k + 1) * HALF)
                act.wait_ge(*xn_ready.after(n, k))
                act.wait_ge(*pe["vv"].after(n - 1, 1))
                act.activation(xn_hi[:, cols_], y[:, cols_], ACT.Copy).then_inc(xn_hi_ready.handle, 1)

            def qq_hi_half(n, k):
                act.wait_ge(*pe["qq"].after(n, k))
                act.wait_ge(*pe["s"].after(n - 1, 7))
                act.activation(qq_hi[:, k * HALF:(k + 1) * HALF], bank("qq", k)[:, :], ACT.Identity, bias=bq1_s) \
                   .then_inc(qq_hi_ready.handle, 1)

            def kk_hi_half(n, k):
                act.wait_ge(*pe["kk"].after(n, k))
                act.activation(kk_hi[:, k * HALF:(k + 1) * HALF], bank("kk", k)[:, :], ACT.Identity, bias=bk1) \
                   .then_inc(kk_hi_ready.handle, 1)

            def vv_hi_half(n, k):
                act.wait_ge(*pe["vv"].after(n, k))
                act.wait_ge(*pe["pv"].after(n - 1, 1))
                act.activation(vv_hi[:, 4 * k:4 * k + 4, :], bank("vv", k)[:, :].rearrange("p (t c) -> p t c", t=4),
                               ACT.Copy).then_inc(vv_hi_ready.handle, 1)

            def residual(n, k):
                act.wait_ge(*pe["xbt"].after(n, k))
                act.wait_ge(*o_ready.after(n - 1, k))
                act.activation(r_tok[:, 4 * k:4 * k + 4, :], bank("xbt", k)[:, :].rearrange("p (t c) -> p t c", t=4),
                               ACT.Copy).then_inc(r_tok_ready.handle, 1)

            def exp(n, t):
                act.wait_ge(*max1_ready.after(n, t))
                act.wait_ge(*pe["t"].after(n, t - 1))
                if t % 4 == 0:
                    act.wait_ge(*rec1_ready.after(n - 1, t // 4))
                act.activation(e[:, :], ps_s[:, :], ACT.Exp, bias=nm1[:, t:t + 1], accum_out=sum1[:, t:t + 1]) \
                   .then_inc(e_ready.handle, 1)

            def et_hi_tile(n, t):
                act.wait_ge(*pe["t"].after(n, t))
                if t % 4 == 0:
                    act.wait_ge(*pe["pv"].after(n, t // 4 - 1))
                act.activation(et_hi[:, :, (t % 4) * 128:(t % 4 + 1) * 128],
                               ps_t[:, :].rearrange("p (k c) -> p k c", k=TILES), ACT.Copy) \
                   .then_inc(et_hi_ready.handle, 1)

            def a_t_half(n, k):
                act.wait_ge(*pe["pv"].after(n, k))
                act.wait_ge(*pe["ft"].after(n, k - 1))
                act.activation(a_t[:, :], bank("pv", k)[:, :], ACT.Copy).then_inc(a_t_ready.handle, 1)

            act.wait_ge(loads, 16 * N_LOADS)
            act.activation(ident_r[:, :], ident, ACT.Copy)
            act.activation(mask_r[:, :], const[:, 128:128 + WIN], ACT.Copy)
            act.activation(bq0_s, b_qkv[:, 0:1], ACT.Copy, scale=SCALE)
            act.activation(bq1_s, bq1, ACT.Copy, scale=SCALE).then_inc(set_act, 1)
            for k in range(12):
                act.wait_ge(set_wc, k + 1)
                act.activation(wc_hi[:, k // 3, k % 3, :], wc_f[:, k % 4, :], ACT.Copy).then_inc(set_act, 1)
            act.wait_ge(set_act, 13)
            act.wait_ge(set_dve, 4)

            def turn_program(turn):
                p0, p1, p2, p3 = (turn.active(k) for k in range(4))
                a, b, c, d = turn.a, turn.b, turn.c, turn.d
                if p3:
                    residual(a, 0)
                    residual(a, 1)
                if p2:
                    local_exp(b, 0)
                if p3:
                    et_hi_tile(a, 0)
                    exp(a, 1)
                if p1:
                    take_m1(c, 0)
                if p3:
                    et_hi_tile(a, 1)
                if p2:
                    pt_hi_pair(b, 0)
                if p3:
                    exp(a, 2)
                if p2:
                    local_exp(b, 1)
                if p1:
                    t_hi_half(c, 1)
                    gelu(c, 0)
                    gelu(c, 1)
                if p3:
                    et_hi_tile(a, 2)
                if p2:
                    pt_hi_pair(b, 1)
                if p3:
                    exp(a, 3)
                if p1:
                    take_m1(c, 1)
                if p2:
                    local_exp(b, 2)
                if p3:
                    et_hi_tile(a, 3)
                    exp(a, 4)
                if p2:
                    pt_hi_pair(b, 2)
                    local_exp(b, 3)
                if p1:
                    h_hi_half(c, 0)
                if p2:
                    pt_hi_pair(b, 3)
                if p1:
                    gelu(c, 2)
                    gelu(c, 3)
                    q_hi_half(c, 0)
                    k_hi_half(c, 0)
                if p3:
                    exp(a, 5)
                if p2:
                    xn_hi_half(b, 0)
                    xn_hi_half(b, 1)
                if p1:
                    v_hi_half(c, 0)
                if p3:
                    a_t_half(a, 0)
                    et_hi_tile(a, 4)
                if p1:
                    h_hi_half(c, 1)
                if p3:
                    et_hi_tile(a, 5)
                    exp(a, 6)
                if p1:
                    q_hi_half(c, 1)
                    k_hi_half(c, 1)
                if p3:
                    et_hi_tile(a, 6)
                    exp(a, 7)
                if p1:
                    v_hi_half(c, 1)
                if p2:
                    qq_hi_half(b, 0)
                    qq_hi_half(b, 1)
                if p3:
                    et_hi_tile(a, 7)
                if p2:
                    kk_hi_half(b, 0)
                    kk_hi_half(b, 1)
                if p0:
                    t_hi_half(d, 0)
                if p3:
                    a_t_half(a, 1)
                if p2:
                    vv_hi_half(b, 0)
                    exp(b, 0)
                    vv_hi_half(b, 1)

            run_turns(act, turn_program)

        @block.gpsimd
        def _(pool):
            def minus(dst, full, hi):
                return pool.tensor_tensor(dst, full, hi, ALU.subtract)

            def transform(n, k):
                rows = [xp[:, k * ROWS + r:k * ROWS + r + ROWS - 1:2, :] for r in range(4)]
                pool.wait_ge(*xp_ready.after(n, 1))
                pool.wait_ge(*t_lo_ready.after(n, k - 1))
                for i, (x, y_, op) in enumerate(((0, 2, ALU.subtract), (1, 2, ALU.add), (2, 1, ALU.subtract),
                                                 (1, 3, ALU.subtract))):
                    ins_ = pool.tensor_tensor(t_f[:, i], rows[x], rows[y_], op)
                ins_.then_inc(t_ready.handle, 1)

            def t_lo_half(n, k):
                pool.wait_ge(*t_hi_ready.after(n, k))
                minus(t_lo[:, :, :, :].rearrange("p i r w -> p (i r w)"), t_f[:, :, :, :].rearrange("p i r w -> p (i r w)"),
                      t_hi[:, :, :, :].rearrange("p i r w -> p (i r w)").bitcast(F32)).then_inc(t_lo_ready.handle, 1)

            def g_lo_part(n, k):
                pool.wait_ge(*g_hi_ready.after(n, k))
                minus(g_lo[:, k % 2, :], g[:, k % 2, :], g_hi[:, k % 2, :].bitcast(F32)) \
                    .then_inc(g_lo_ready.handle, 1)

            def h_lo_half(n, k):
                cols_ = slice(k * HALF, (k + 1) * HALF)
                pool.wait_ge(*h_hi_ready.after(n, k))
                minus(h_lo[:, cols_], h[:, cols_], h_hi[:, cols_].bitcast(F32)).then_inc(h_lo_ready.handle, 1)

            def v_lo_half(n, k):
                pool.wait_ge(*v_hi_ready.after(n, k))
                minus(v_hl[:, 4 * k:4 * k + 4, 1, :], v_full[:, :, :], v_hl[:, 4 * k:4 * k + 4, 0, :].bitcast(F32)) \
                    .then_inc(v_lo_ready.handle, 1)

            def xn_lo_half(n, k):
                cols_ = slice(k * HALF, (k + 1) * HALF)
                pool.wait_ge(*xn_hi_ready.after(n, k))
                minus(xn_lo[:, cols_], y[:, cols_], xn_hi[:, cols_].bitcast(F32)).then_inc(xn_lo_ready.handle, 1)

            pool.memset(xp[:, :, :], 0.0)
            for t in (kp_hi, kp_lo):
                pool.memset(t[:, :, :].bitcast(F32), 0.0)
            pool.memset(v_halo[:, :, :, :].bitcast(F32), 0.0)
            pool.memset(pn_halo[:, :], 0.0)
            pool.memset(minus_half[:, :], -0.5).then_inc(set_pool, 1)
            pool.wait_ge(set_pool, 1)
            for k in range(12):
                pool.wait_ge(set_act, k + 2)
                minus(wc_lo[:, k // 3, k % 3, :], wc_f[:, k % 4, :], wc_hi[:, k // 3, k % 3, :].bitcast(F32)) \
                    .then_inc(set_pool, 1)

            def turn_program(turn):
                p0, p1, p2, p3 = (turn.active(k) for k in range(4))
                b, c, d = turn.b, turn.c, turn.d
                if p1:
                    transform(c, 1)
                    t_lo_half(c, 1)
                    g_lo_part(c, 0)
                    g_lo_part(c, 1)
                    h_lo_half(c, 0)
                    g_lo_part(c, 2)
                    g_lo_part(c, 3)
                if p2:
                    pool.wait_ge(*gn_step.after(b, 4))
                    pool.tensor_tensor(rstd, var_eps, minus_half[:, :], ALU.pow).then_inc(rstd_ready.handle, 1)
                if p1:
                    v_lo_half(c, 0)
                if p2:
                    xn_lo_half(b, 0)
                    xn_lo_half(b, 1)
                if p1:
                    h_lo_half(c, 1)
                if p0:
                    transform(d, 0)
                if p1:
                    v_lo_half(c, 1)
                if p0:
                    t_lo_half(d, 0)

            run_turns(pool, turn_program)

        @block.vector
        def _(dve):
            def x_half(n, k):
                dve.wait_ge(*pe["xt"].after(n, k))
                dve.wait_ge(*t_ready.after(n - 1, 1))
                dve.wait_ge(*h_ready.after(n - 1, 1))
                dve.tensor_copy(inside(xp, k), bank("xt", k)[:, :].rearrange("p (r w) -> p r w", r=ROWS)) \
                   .then_inc(xp_ready.handle, 1)

            def conv_rows(n, half, s):
                pos, dst, src, op = ((1, 1, 0, ALU.subtract), (1, 0, 0, ALU.add), (2, 0, 0, ALU.add),
                                     (3, 1, 1, ALU.subtract))[s - 1]
                dve.wait_ge(*pe["conv"].after(n, 4 * half + pos))
                dve.wait_ge(*u_step.after(n, 5 * half + s - 1))
                dve.tensor_tensor(u[:, :, :, dst, :], u[:, :, :, src, :], bank("conv", 4 * half + pos)[:, :]
                                  .rearrange("p (m r w) -> p m r w", m=2, r=PAIRS), op).then_inc(u_step.handle, 1)

            def g_hi_part(n, k):
                dve.wait_ge(*g_ready.after(n, k))
                dve.wait_ge(*pe["up2"].after(n, k // 2 - 1))
                dve.tensor_copy(g_hi[:, k % 2, :], g[:, k % 2, :]).then_inc(g_hi_ready.handle, 1)

            def h_half(n, k):
                cols_ = slice(k * HALF, (k + 1) * HALF)
                dve.wait_ge(*pe["up2"].after(n, k))
                dve.wait_ge(*h_lo_ready.after(n - 1, k))
                dve.scalar_tensor_tensor(h[:, cols_].rearrange("p (r w) -> p r w", r=ROWS),
                                         bank("up2", k)[:, :].rearrange("p (r w) -> p r w", r=ROWS), b_up2,
                                         inside(xp, k), ALU.add, ALU.add) \
                   .then_inc(h_ready.handle, 1)

            def biased_lo(dst, src, bias, hi):
                return dve.scalar_tensor_tensor(dst, src, bias, hi, ALU.add, ALU.subtract)

            def q_lo_half(n, k):
                cols_ = slice(k * HALF, (k + 1) * HALF)
                dve.wait_ge(*q_hi_ready.after(n, k))
                biased_lo(q_lo[:, cols_], bank("q", k)[:, :], bq0_s, q_hi[:, cols_].bitcast(F32)) \
                    .then_inc(q_lo_ready.handle, 1)

            def k_lo_half(n, k):
                inside = (slice(None), slice(1 + k * ROWS, 1 + (k + 1) * ROWS), slice(1, 1 + W))
                dve.wait_ge(*k_hi_ready.after(n, k))
                biased_lo(kp_lo[inside], bank("k", k)[:, :].rearrange("p (r w) -> p r w", r=ROWS),
                          b_qkv[:, 1:2], kp_hi[inside].bitcast(F32)).then_inc(k_lo_ready.handle, 1)

            def v_half(n, k):
                dve.wait_ge(*pe["v"].after(n, k))
                dve.wait_ge(*v_lo_ready.after(n, k - 1))
                dve.tensor_tensor(v_full[:, :, :], bank("v", k)[:, :].rearrange("p (t c) -> p t c", t=4),
                                  bv0_row[:, :].rearrange("p (a c) -> p a c", a=1).broadcast_to([128, 4, 128]),
                                  ALU.add).then_inc(v_ready.handle, 1)

            def local_max(n, j):
                dve.wait_ge(*pe["as"].after(n, j))
                dve.wait_ge(*p0_ready.after(n - 1, j))
                dve.tensor_reduce(nm0[:, 2 * j:2 * j + 2], bank("as", j)[:, 0:2 * WIN]
                                  .rearrange("p (u k) -> p u k", u=2), AX.X, ALU.max, negate=True) \
                   .then_inc(max0_ready.handle, 1)

            def local_norm(n, j):
                dve.wait_ge(*p0_ready.after(n, j))
                dve.reciprocal(rec0[:, 2 * j:2 * j + 2], sum0[:, 2 * j:2 * j + 2]).then_inc(rec0_ready.handle, 1)
                dve.wait_ge(*rec0_ready.after(n, j))
                dve.wait_ge(*pe["at"].after(n, j - 1))
                pair = p0[:, 2 * (j % 2):2 * (j % 2) + 2]
                rec = rec0[:, 2 * j:2 * j + 2].rearrange("p (u r w) -> p u r w", r=1, w=1)
                dve.tensor_tensor(pn_own[:, :, :].rearrange("p u (r w) -> p u r w", r=4), pair[:, :, 1:5, 1:1 + W],
                                  rec.broadcast_to([128, 2, 4, W]), ALU.mult)
                halo = pn_halo[:, :].rearrange("p (u x) -> p u x", u=2)[:, :, 0:64].rearrange("p u (r w) -> p u r w", r=2)
                ins_ = dve.tensor_tensor(halo, pair[:, :, 0:6:5, 1:1 + W], rec.broadcast_to([128, 2, 2, W]), ALU.mult)
                ins_.then_inc(p0n_ready.handle, 1)

            def pt_lo_pair(n, j):
                dve.wait_ge(*pt_hi_ready.after(n, j))
                dve.tensor_tensor(pt_lo[:, :, :], bank("at", j)[:, :].rearrange("p (u c) -> p u c", u=4),
                                  pt_hi[:, :, :].bitcast(F32), ALU.subtract).then_inc(pt_lo_ready.handle, 1)

            def y_pair(n, j):
                cols_ = slice(j * 256, (j + 1) * 256)
                dve.wait_ge(*pe["av"].after(n, j))
                dve.wait_ge(*pe["xbt"].after(n - 1, j // 2))
                dve.tensor_tensor(y[:, cols_], bank("av", j)[:, 0:256], h[:, cols_], ALU.add) \
                   .then_inc(y_ready.handle, 1)
                dve.wait_ge(*y_ready.after(n, j))
                dve.bn_stats(stats[:, j, :], y[:, cols_]).then_inc(stat_ready.handle, 1)

            def channel_moments(n):
                dve.bn_aggr(moments[:, :], stats[:, :, :].rearrange("p a s -> p (a s)")).then_inc(gn_step.handle, 1)
                dve.wait_ge(*gn_step.after(n, 0))
                dve.scalar_tensor_tensor(moments[:, 1:2], moments[:, 0:1], moments[:, 0:1], moments[:, 1:2],
                                         ALU.mult, ALU.add).then_inc(gn_step.handle, 1)

            def group_norm(n):
                dve.wait_ge(*pe["gn"].after(n, 0))
                dve.tensor_copy(g_mom[:, :], bank("gn", 0)[:, 0:2]).then_inc(gn_step.handle, 1)
                dve.wait_ge(*gn_step.after(n, 2))
                dve.scalar_tensor_tensor(neg_var, g_mom[:, 0:1], g_mom[:, 0:1], g_mom[:, 1:2],
                                         ALU.mult, ALU.subtract).then_inc(gn_step.handle, 1)
                dve.wait_ge(*gn_step.after(n, 3))
                dve.tensor_scalar(var_eps, neg_var, -1.0, EPS, ALU.mult, ALU.add).then_inc(gn_step.handle, 1)
                dve.wait_ge(*rstd_ready.after(n, 0))
                dve.tensor_tensor(gn_a, gamma, rstd, ALU.mult).then_inc(gn_step.handle, 1)
                dve.wait_ge(*gn_step.after(n, 5))
                dve.scalar_tensor_tensor(gn_nb, g_mom[:, 0:1], gn_a, beta, ALU.mult, ALU.subtract) \
                   .then_inc(gn_step.handle, 1)
                dve.wait_ge(*gn_step.after(n, 6))
                for k in range(2):
                    cols_ = slice(k * HALF, (k + 1) * HALF)
                    dve.tensor_scalar(y[:, cols_], y[:, cols_], gn_a, gn_nb, ALU.mult, ALU.subtract) \
                       .then_inc(xn_ready.handle, 1)

            def residual_bias(n, k):
                cols_ = slice(k * HALF, (k + 1) * HALF)
                dve.wait_ge(*xn_lo_ready.after(n, k))
                dve.tensor_scalar(y[:, cols_], y[:, cols_], b_tot, None, ALU.add).then_inc(xb_ready.handle, 1)

            def qq_lo_half(n, k):
                cols_ = slice(k * HALF, (k + 1) * HALF)
                dve.wait_ge(*qq_hi_ready.after(n, k))
                biased_lo(qq_lo[:, cols_], bank("qq", k)[:, :], bq1_s, qq_hi[:, cols_].bitcast(F32)) \
                    .then_inc(qq_lo_ready.handle, 1)

            def kk_lo_half(n, k):
                cols_ = slice(k * HALF, (k + 1) * HALF)
                dve.wait_ge(*kk_hi_ready.after(n, k))
                biased_lo(kk_lo[:, cols_], bank("kk", k)[:, :], bk1, kk_hi[:, cols_].bitcast(F32)) \
                    .then_inc(kk_lo_ready.handle, 1)

            def vv_lo_half(n, k):
                dve.wait_ge(*vv_hi_ready.after(n, k))
                dve.tensor_tensor(vv_lo[:, 4 * k:4 * k + 4, :], bank("vv", k)[:, :].rearrange("p (t c) -> p t c", t=4),
                                  vv_hi[:, 4 * k:4 * k + 4, :].bitcast(F32), ALU.subtract) \
                   .then_inc(vv_lo_ready.handle, 1)

            def row_max(n, t):
                dve.wait_ge(*pe["s"].after(n, t))
                dve.wait_ge(*e_ready.after(n - 1, t))
                dve.tensor_reduce(nm1[:, t:t + 1], ps_s[:, :], AX.X, ALU.max, negate=True) \
                   .then_inc(max1_ready.handle, 1)

            def et_lo_tile(n, t):
                cols_ = slice((t % 4) * 128, (t % 4 + 1) * 128)
                dve.wait_ge(*et_hi_ready.after(n, t))
                dve.tensor_tensor(et_lo[:, :, cols_], ps_t[:, :].rearrange("p (k c) -> p k c", k=TILES),
                                  et_hi[:, :, cols_].bitcast(F32), ALU.subtract).then_inc(et_lo_ready.handle, 1)

            def output(n, k):
                four = slice(4 * k, 4 * k + 4)
                dve.wait_ge(*e_ready.after(n, 4 * k + 3))
                dve.reciprocal(rec1[:, four], sum1[:, four]).then_inc(rec1_ready.handle, 1)
                dve.wait_ge(*rec1_ready.after(n, k))
                dve.wait_ge(*pe["ft"].after(n, k))
                dve.wait_ge(*r_tok_ready.after(n, k))
                dve.wait_ge(*stored.after(n, k - 1))
                for t in range(4):
                    ins_ = dve.scalar_tensor_tensor(o_sb[:, t, :], bank("ft", k)[:, t * 128:(t + 1) * 128],
                                                    rec1[:, 4 * k + t:4 * k + t + 1], r_tok[:, 4 * k + t, :],
                                                    ALU.mult, ALU.add)
                ins_.then_inc(o_ready.handle, 1)

            own = ctx.enter_context(nc.semaphore("set_own"))
            done = [0]

            def step(ins_):
                ins_.then_inc(own, 1)
                done[0] += 1
                dve.wait_ge(own, done[0])

            def split(hi, lo, full):
                step(dve.tensor_copy(hi, full))
                dve.tensor_tensor(lo, full, hi.bitcast(F32), ALU.subtract)

            dve.wait_ge(loads, 16 * N_LOADS)
            dve.wait_ge(set_pe, 1)
            dve.tensor_copy(w_up1_t, ps_s[:, 0:768].rearrange("p (j d) -> p j d", j=3)).then_inc(set_dve, 1)
            dve.wait_ge(set_pe, 2)
            dve.tensor_copy(wv_t, work[0][:, 256:384]).then_inc(set_dve, 1)
            split(w2_hi[:, :, :], w2_lo[:, :, :], work[0][:, 0:256].rearrange("p (m c) -> p m c", m=2))
            dve.wait_ge(set_pe, 3)
            step(dve.tensor_copy(w_qkv, work[1][:, 0:384].rearrange("p (m c) -> p m c", m=3)))
            step(dve.tensor_scalar(w_qkv[:, 0, :], w_qkv[:, 0, :], SCALE, None, ALU.mult))
            split(w0_hi[:, :, :], w0_lo[:, :, :], w_qkv)
            step(dve.tensor_scalar(wl1[:, 0, :], wl1[:, 0, :], SCALE, None, ALU.mult))
            split(w1_hi[:, 0:2, :], w1_lo[:, 0:2, :], wl1[:, 0:2, :])
            dve.wait_ge(set_dve, 2)
            step(dve.tensor_copy(wperc_g[:, :, 0:4:3, :], wperc[:, :, 0:3:2, :]))
            step(dve.tensor_tensor(wperc_g[:, :, 1, :], wperc[:, :, 0, :], wperc[:, :, 2, :], ALU.add))
            step(dve.tensor_tensor(wperc_g[:, :, 2, :], wperc_g[:, :, 1, :], wperc[:, :, 1, :], ALU.subtract))
            step(dve.tensor_tensor(wperc_g[:, :, 1, :], wperc_g[:, :, 1, :], wperc[:, :, 1, :], ALU.add))
            step(dve.tensor_scalar(wperc_g[:, :, 1:3, :], wperc_g[:, :, 1:3, :], 0.5, None, ALU.mult))
            for k in range(12):
                i, dx = k // 3, k % 3
                acc = wc_f[:, k % 4, :]
                if k >= 4:
                    dve.wait_ge(set_pool, k - 2)
                step(dve.tensor_scalar(acc, w_up1_t[:, 0, :], wperc_g[:, 0, i, dx:dx + 1], None, ALU.mult))
                step(dve.scalar_tensor_tensor(acc, w_up1_t[:, 1, :], wperc_g[:, 1, i, dx:dx + 1], acc, ALU.mult, ALU.add))
                dve.scalar_tensor_tensor(acc, w_up1_t[:, 2, :], wperc_g[:, 2, i, dx:dx + 1], acc, ALU.mult, ALU.add) \
                   .then_inc(set_wc, 1)
            dve.wait_ge(set_pe, 4)
            step(dve.tensor_copy(wvp, work[2][:, 0:128]))
            split(w1_hi[:, 2, :], w1_lo[:, 2, :], wvp)
            dve.tensor_tensor(b_tot, work[2][:, 128:129], bp1, ALU.add)
            dve.tensor_tensor(b_hid, work[2][:, 129:131], b_up1, ALU.add).then_inc(set_dve, 1)
            dve.wait_ge(set_dve, 3)
            dve.wait_ge(set_act, 1)
            dve.memset(neg_var, 0.0).then_inc(set_dve, 1)

            def turn_program(turn):
                p0, p1, p2, p3 = (turn.active(k) for k in range(4))
                a, b, c, d = turn.a, turn.b, turn.c, turn.d
                if p2:
                    local_max(b, 0)
                if p3:
                    row_max(a, 1)
                if p2:
                    local_norm(b, 0)
                if p3:
                    et_lo_tile(a, 0)
                if p1:
                    conv_rows(c, 0, 1)
                    conv_rows(c, 0, 2)
                if p3:
                    row_max(a, 2)
                    et_lo_tile(a, 1)
                if p2:
                    local_max(b, 1)
                    pt_lo_pair(b, 0)
                if p1:
                    conv_rows(c, 0, 3)
                if p2:
                    local_norm(b, 1)
                if p1:
                    conv_rows(c, 0, 4)
                if p2:
                    y_pair(b, 0)
                if p3:
                    row_max(a, 3)
                if p1:
                    g_hi_part(c, 0)
                    g_hi_part(c, 1)
                if p3:
                    et_lo_tile(a, 2)
                if p2:
                    local_max(b, 2)
                    pt_lo_pair(b, 1)
                if p1:
                    conv_rows(c, 1, 1)
                    conv_rows(c, 1, 2)
                if p2:
                    local_norm(b, 2)
                if p2:
                    y_pair(b, 1)
                if p3:
                    row_max(a, 4)
                    et_lo_tile(a, 3)
                if p2:
                    local_max(b, 3)
                    pt_lo_pair(b, 2)
                if p1:
                    h_half(c, 0)
                if p2:
                    local_norm(b, 3)
                if p1:
                    conv_rows(c, 1, 3)
                    conv_rows(c, 1, 4)
                if p2:
                    y_pair(b, 2)
                    pt_lo_pair(b, 3)
                if p3:
                    row_max(a, 5)
                if p1:
                    g_hi_part(c, 2)
                if p2:
                    y_pair(b, 3)
                    dve.wait_ge(*stat_ready.after(b, 3))
                if p1:
                    g_hi_part(c, 3)
                if p2:
                    channel_moments(b)
                if p1:
                    q_lo_half(c, 0)
                    k_lo_half(c, 0)
                    v_half(c, 0)
                if p2:
                    group_norm(b)
                if p3:
                    et_lo_tile(a, 4)
                if p1:
                    h_half(c, 1)
                if p3:
                    row_max(a, 6)
                if p0:
                    x_half(d, 0)
                    x_half(d, 1)
                if p3:
                    et_lo_tile(a, 5)
                if p1:
                    q_lo_half(c, 1)
                    k_lo_half(c, 1)
                if p3:
                    row_max(a, 7)
                    et_lo_tile(a, 6)
                    output(a, 0)
                if p1:
                    v_half(c, 1)
                if p2:
                    qq_lo_half(b, 0)
                    qq_lo_half(b, 1)
                if p3:
                    et_lo_tile(a, 7)
                if p2:
                    kk_lo_half(b, 0)
                    kk_lo_half(b, 1)
                    residual_bias(b, 0)
                    residual_bias(b, 1)
                    row_max(b, 0)
                    vv_lo_half(b, 0)
                if p3:
                    output(a, 1)
                if p2:
                    vv_lo_half(b, 1)

            run_turns(dve, turn_program)


_INS = ["x", "L0_conv_w_perc", "L0_conv_w_up1", "L0_conv_w_up2", "L0_conv_w_qkv", "L0_conv_b_qkv",
        "L1_conv_Wq", "L1_conv_Wk", "L1_conv_Wv", "L1_conv_Wp"]
_COLS = [("L0_conv_b_perc", 3), ("L0_conv_b_up1", 2), ("L0_conv_b_up2", 1), ("L0_conv_b_qkv", 3), ("L1_conv_gamma", 1),
         ("L1_conv_beta", 1), ("L1_conv_bq", 1), ("L1_conv_bk", 1), ("L1_conv_bv", 1), ("L1_conv_bp", 1)]


def kernel(**inputs):
    import numpy as np
    import concourse.bacc as bacc
    from concourse.bass_utils import run_bass_kernel_spmd

    const = np.zeros((128, CONST_W), np.float32)
    const[:, 0:128] = np.eye(128)
    row, col = np.arange(128) // W, np.arange(128) % W
    key_row, key_col = np.arange(WIN) // WP, np.arange(WIN) % WP
    dy, dx = key_row[None] - row[:, None], key_col[None] - col[:, None]
    const[:, 128:128 + WIN] = np.where((dy >= 0) & (dy <= 2) & (dx >= 0) & (dx <= 2), 0.0, MASKED)
    groups = np.arange(128) // GROUP
    const[:, 128 + WIN:] = (groups[:, None] == groups[None]) / GROUP

    nc = bacc.Bacc("TRN2", target_bir_lowering=False, num_devices=1)
    arrays, views = {}, {}
    cols = [np.asarray(inputs[name]).reshape(128, k) if name == "L0_conv_b_perc"
            else np.asarray(inputs[name]).reshape(k, 128).T for name, k in _COLS]
    extra = {"const": const, "cols": np.ascontiguousarray(np.concatenate(cols, axis=1))}
    for name in _INS + ["const", "cols"]:
        array = extra[name] if name in extra else np.ascontiguousarray(inputs[name])
        arrays[f"in_{name}"] = array
        views[name] = nc.dram_tensor(f"in_{name}", array.shape, mybir.dt.from_np(array.dtype), kind="ExternalInput").ap()
    out = nc.dram_tensor("out", (B, H, W, C), F32, kind="ExternalOutput").ap()
    conv_seq_kernel(nc, views, out)
    result = run_bass_kernel_spmd(nc, [arrays], core_ids=[0])
    return result.results[0]["out"]
```

```python
from contextlib import ExitStack

import concourse.bass as bass
from concourse import mybir

F32 = mybir.dt.float32
F32R = mybir.dt.float32r
ALU = mybir.AluOpType
ACT = mybir.ActivationFunctionType
AX = mybir.AxisListType

B, H, W, C = 16, 32, 32, 128
PIX = H * W
TILES = PIX // 128
HALF = PIX // 2
ROWS = H // 2
HP, WP = H + 2, W + 2
PAIRS = ROWS // 2
WINO = (1, 2, 0, 3)
T_PART = (slice(1, 3), slice(0, 4, 3))
WIN = 6 * WP
D = 2 * C
GROUP = C // 8
EPS = 1e-3
SCALE = float(C) ** -0.5
MASKED = -1e30
CONST_W = 128 + WIN + 128


class Count:

    def __init__(self, handle, per_image, unit=1):
        self.handle, self.per_image, self.unit = handle, per_image, unit

    def after(self, n, e):
        value = n * (self.per_image * self.unit) + (e + 1) * self.unit
        return self.handle, max(value, 0) if isinstance(value, int) else value


BANK_PLAN = [
    ("xbt", 0, 0), ("xbt", 1, 3), ("as", 0, 2), ("conv", 0, 0), ("conv", 1, 3), ("at", 0, 0),
    ("as", 1, 1), ("conv", 2, 2), ("conv", 3, 3), ("av", 0, 0), ("at", 1, 3), ("as", 2, 2),
    ("conv", 4, 0), ("conv", 5, 1), ("av", 1, 3), ("at", 2, 2), ("as", 3, 0), ("up2", 0, 1),
    ("conv", 6, 3), ("conv", 7, 2), ("av", 2, 1), ("at", 3, 3), ("pv", 0, 0), ("av", 3, 3),
    ("q", 0, 1), ("k", 0, 0), ("v", 0, 2), ("gn", 0, 3), ("up2", 1, 1), ("pv", 1, 0),
    ("xt", 0, 3), ("xt", 1, 2), ("q", 1, 1), ("k", 1, 3), ("ft", 0, 0), ("pv", 2, 2),
    ("v", 1, 1), ("qq", 0, 3), ("kk", 0, 2), ("qq", 1, 0), ("kk", 1, 1), ("vv", 0, 3),
    ("pv", 3, 0), ("ft", 1, 2), ("vv", 1, 1),
]
BANK_OF = {(u, e): bank for u, e, bank in BANK_PLAN}
LAST_PLAN = [("xbt", 0, 2), ("xbt", 1, 3), ("pv", 0, 2), ("pv", 1, 3), ("ft", 0, 2), ("pv", 2, 3), ("pv", 3, 2), ("ft", 1, 3)]
LAST_BANK_OF = {(u, e): bank for u, e, bank in LAST_PLAN}
STAGE_OF = dict(xt=0, conv=1, up2=1, q=1, k=1, v=1, av=2, at=2, gn=2, qq=2, kk=2, vv=2, xbt=3, pv=3, ft=3)
STAGE_OF["as"] = 2


def is_last(n):
    return isinstance(n, int) and n == B - 1


class Turn:

    def __init__(self, it):
        self.it = it
        self.a, self.b, self.c, self.d = it, it + 1, it + 2, it + 3
        self.fixed = isinstance(it, int)

    def active(self, stage, back=0):
        if not self.fixed:
            return True
        return 0 <= self.it - back + 3 - stage < B

    def previous_user(self, user, e):
        plan = LAST_PLAN if is_last(self.it) else BANK_PLAN
        at = [(u, x) for u, x, _ in plan].index((user, e))
        return self.last_user(plan[at][2], [(u, x, b) for u, x, b in plan[:at]]) or (user, -1, 0)

    def last_user(self, bank, earlier_in_turn=()):
        before = [(u, x, 0) for u, x, b in earlier_in_turn if b == bank][::-1]
        whole = [(u, x) for u, x, b in BANK_PLAN if b == bank][::-1]
        for back in range(1, 5):
            before += [(u, x, back) for u, x in whole]
        for u, x, back in before:
            if self.active(STAGE_OF[u], back):
                return u, x, self.it - back + 3 - STAGE_OF[u]
        return None


def conv_seq_kernel(nc, ins, out):
    ctx = ExitStack()
    with ctx:
        def sb(name, shape, dt=F32):
            return ctx.enter_context(nc.sbuf_tensor(name, shape, dt))

        def count(name, per_image, unit=1):
            return Count(ctx.enter_context(nc.semaphore(name)), per_image, unit)

        const = sb("const", [128, CONST_W])
        ident, mask, group_avg = const[:, 0:128], const[:, 128:128 + WIN], const[:, 128 + WIN:CONST_W]
        minus_half = sb("minus_half", [128, 1])
        wperc = sb("wperc", [128, 3, 3, 3])
        wperc_g = sb("wperc_g", [128, 3, 4, 3])
        cols = sb("cols", [128, 24])
        b_perc, b_up1, b_up2, b_qkv = cols[:, 0:3], cols[:, 3:5], cols[:, 5:6], cols[:, 6:9]
        gamma, beta, bq1, bk1, bv1, bp1 = (cols[:, 9 + k:10 + k] for k in range(6))
        b_hid, bq0_s, bq1_s, b_tot = cols[:, 15:17], cols[:, 17:18], cols[:, 18:19], cols[:, 19:20]
        bv0_row = sb("bv0_row", [128, 128])
        wc_hi, wc_lo = (sb(f"wc_{p}", [128, 4, 3, D], F32R) for p in ("hi", "lo"))
        w2_hi, w2_lo = (sb(f"w2_{p}", [128, 2, 128], F32R) for p in ("hi", "lo"))
        w0_hi, w0_lo = (sb(f"w0_{p}", [128, 3, 128], F32R) for p in ("hi", "lo"))
        w1_hi, w1_lo = (sb(f"w1_{p}", [128, 3, 128], F32R) for p in ("hi", "lo"))

        x_in = sb("x_in", [128, TILES, 128])
        xp = sb("xp", [128, HP, WP])
        t_f = sb("t_f", [128, 4, PAIRS, WP])
        t_hi, t_lo = (sb(f"t_{p}", [128, 4, PAIRS, WP], F32R) for p in ("hi", "lo"))
        u = sb("u", [128, 2, PAIRS, 2, W])
        g = sb("g", [128, 2, HALF])
        g_hi, g_lo = (sb(f"g_{p}", [128, 2, HALF], F32R) for p in ("hi", "lo"))
        h = sb("h", [128, PIX])
        h_hi, h_lo = (sb(f"h_{p}", [128, PIX], F32R) for p in ("hi", "lo"))
        q_hi, q_lo = (sb(f"q_{p}", [128, PIX], F32R) for p in ("hi", "lo"))
        kp_hi, kp_lo = (sb(f"kp_{p}", [128, HP, WP], F32R) for p in ("hi", "lo"))
        v_full = sb("v_full", [128, 4, 128])
        v_hl = sb("v_hl", [128, TILES, 2, 128], F32R)
        v_halo = sb("v_halo", [128, TILES // 2, 2, 128], F32R)

        nm0 = sb("nm0", [128, TILES])
        sum0 = sb("sum0", [128, TILES])
        rec0 = sb("rec0", [128, TILES])
        p0 = sb("p0", [128, 4, 6, WP])
        pn_own = sb("pn_own", [128, 2, 128])
        pn_halo = sb("pn_halo", [128, 384])
        pt_hi, pt_lo = (sb(f"pt_{p}", [128, 4, 128], F32R) for p in ("hi", "lo"))
        y = sb("y", [128, PIX])
        stats = sb("stats", [128, 4, 6])
        moments = sb("moments", [128, 2])
        g_mom = sb("g_mom", [128, 2])
        gn = sb("gn", [128, 5])
        neg_var, var_eps, rstd, gn_a, gn_nb = (gn[:, k:k + 1] for k in range(5))
        xn_hi, xn_lo = (sb(f"xn_{p}", [128, PIX], F32R) for p in ("hi", "lo"))

        qq_hi, qq_lo = (sb(f"qq_{p}", [128, PIX], F32R) for p in ("hi", "lo"))
        kk_hi, kk_lo = (sb(f"kk_{p}", [128, PIX], F32R) for p in ("hi", "lo"))
        vv_hi, vv_lo = (sb(f"vv_{p}", [128, TILES, 128], F32R) for p in ("hi", "lo"))
        nm1 = sb("nm1", [128, TILES])
        sum1 = sb("sum1", [128, TILES])
        rec1 = sb("rec1", [128, TILES])
        e = sb("e", [128, PIX])
        et_hi, et_lo = (sb(f"et_{p}", [128, TILES, HALF], F32R) for p in ("hi", "lo"))
        r_tok = sb("r_tok", [128, TILES, 128])
        a_t = sb("a_t", [128, HALF])
        o_sb = sb("o_sb", [128, 4, 128])

        ps_s = ctx.enter_context(nc.psum_tensor("ps_s", [128, PIX], F32))
        ps_t = ctx.enter_context(nc.psum_tensor("ps_t", [128, PIX], F32))
        work_all = ctx.enter_context(nc.psum_tensor("work", [128, 4 * HALF], F32))
        work = [work_all[:, k * HALF:(k + 1) * HALF] for k in range(4)]

        def bank(user, idx, n=None):
            return work[LAST_BANK_OF[user, idx] if is_last(n) else BANK_OF[user, idx]]

        def score_tile(n, t):
            return work_all[:, 0:PIX] if is_last(n) and t % 2 else ps_s

        x_loaded = count("x_loaded", 1, 16)
        halo_loaded = count("halo_loaded", 4, 16)
        stored = count("stored", 2, 16)
        pe = {u: count(f"pe_{u}", k) for u, k in dict(
            xt=2, conv=8, up2=2, q=2, k=2, v=2, av=4, at=4, gn=1, qq=2, kk=2, vv=2, xbt=2, pv=4,
            ft=2, s=8, t=8).items()}
        pe["as"] = count("pe_as", 4)
        xp_ready, t_ready = count("xp_ready", 2), count("t_ready", 2)
        t_hi_ready, t_lo_ready = count("t_hi_ready", 4), count("t_lo_ready", 4)
        u_step = count("u_step", 10)
        g_ready, g_hi_ready, g_lo_ready = count("g_ready", 4), count("g_hi_ready", 4), count("g_lo_ready", 4)
        h_ready, h_hi_ready, h_lo_ready = count("h_ready", 2), count("h_hi_ready", 2), count("h_lo_ready", 2)
        q_hi_ready, q_lo_ready = count("q_hi_ready", 2), count("q_lo_ready", 2)
        k_hi_ready, k_lo_ready = count("k_hi_ready", 2), count("k_lo_ready", 2)
        v_ready, v_hi_ready, v_lo_ready = count("v_ready", 2), count("v_hi_ready", 2), count("v_lo_ready", 2)
        masked_ready = count("masked_ready", 4)
        max0_ready, p0_ready, rec0_ready, p0n_ready = (
            count("max0_ready", 4), count("p0_ready", 4), count("rec0_ready", 4), count("p0n_ready", 4))
        pt_hi_ready, pt_lo_ready = count("pt_hi_ready", 4), count("pt_lo_ready", 4)
        y_ready, stat_ready = count("y_ready", 4), count("stat_ready", 4)
        gn_step = count("gn_step", 7)
        rstd_ready = count("rstd_ready", 1)
        xn_ready, xn_hi_ready, xn_lo_ready, xb_ready = (
            count("xn_ready", 2), count("xn_hi_ready", 2), count("xn_lo_ready", 2), count("xb_ready", 2))
        qq_hi_ready, qq_lo_ready = count("qq_hi_ready", 2), count("qq_lo_ready", 2)
        kk_hi_ready, kk_lo_ready = count("kk_hi_ready", 2), count("kk_lo_ready", 2)
        vv_hi_ready, vv_lo_ready = count("vv_hi_ready", 2), count("vv_lo_ready", 2)
        r_tok_ready = count("r_tok_ready", 2)
        max1_ready, e_ready, et_hi_ready, et_lo_ready = (
            count("max1_ready", 8), count("e_ready", 8), count("et_hi_ready", 8), count("et_lo_ready", 8))
        a_t_ready, rec1_ready, o_ready = count("a_t_ready", 4), count("rec1_ready", 2), count("o_ready", 2)
        loads_first = ctx.enter_context(nc.semaphore("loads_first"))
        loads = ctx.enter_context(nc.semaphore("loads"))
        set_pe = ctx.enter_context(nc.semaphore("set_pe"))
        set_dve = ctx.enter_context(nc.semaphore("set_dve"))
        set_act = ctx.enter_context(nc.semaphore("set_act"))
        set_pool = ctx.enter_context(nc.semaphore("set_pool"))
        set_first = ctx.enter_context(nc.semaphore("set_first"))
        set_wc = ctx.enter_context(nc.semaphore("set_wc"))

        FREED_BY = dict(xt=xp_ready, conv=u_step, up2=h_ready, q=q_lo_ready, k=k_lo_ready, v=v_ready,
                        at=pt_lo_ready, av=y_ready, gn=gn_step, qq=qq_lo_ready, kk=kk_lo_ready,
                        vv=vv_lo_ready, xbt=r_tok_ready, pv=a_t_ready, ft=o_ready)
        FREED_BY["as"] = masked_ready

        def bank_free(turn, user, idx):
            return read_by(*turn.previous_user(user, idx))

        def read_by(u, x, n):
            if x >= 0 and u == "gn":
                x = 2
            if x >= 0 and u == "conv":
                x = 5 * (x // 4) + (0, 2, 3, 4)[x % 4]
            return FREED_BY[u].after(n, x)

        def inside(padded, half):
            return padded[:, 1 + half * ROWS:1 + (half + 1) * ROWS, 1:1 + W]

        x_view = ins["x"].rearrange("b (t r) w c -> (r w) (b t) c", r=4)
        out_view = out.rearrange("b (t r) w c -> (r w) (b t) c", r=4)

        w_up1 = e[:, 0:768].rearrange("p (m f) -> p m f", m=2)
        w_up1_t = g[:, :, :].rearrange("p m f -> p (m f)")[:, 0:768].rearrange("p (j d) -> p j d", j=3)
        wc_f = [t[:, k * D:(k + 1) * D] for t in (h, e) for k in range(4)]
        w_up2 = y[:, 0:256]
        w_qkv = y[:, 256:640].rearrange("p (m c) -> p m c", m=3)
        wv_t, wvp = y[:, 640:768], y[:, 768:896]
        wl1 = r_tok[:, 0:4, :]

        block = ctx.enter_context(nc.Block())
        N_LOADS_FIRST, N_LOADS = 4, 7

        def run_turns(eng, turn_program):
            for it in (-2, -1, 0):
                turn_program(Turn(it))
            with eng.Fori(1, B - 3) as i:
                turn_program(Turn(i))
            for it in (B - 3, B - 2, B - 1):
                turn_program(Turn(it))

        @block.sync
        def _(sp):
            def load(dst, src, loaded):
                sp.dma_start(dst, src).then_inc(loaded, 16)

            load(w_up1, ins["L0_conv_w_up1"].rearrange("(m p) f a b -> p m (f a b)", m=2), loads_first)
            load(x_in[:, :, :], x_view[:, 0:TILES, :], x_loaded.handle)
            load(w_qkv, ins["L0_conv_w_qkv"].rearrange("(m p) c -> p m c", m=3), loads)
            load(bv0_row[:, :], ins["L0_conv_b_qkv"][2 * C:3 * C].rearrange("(a c) -> a c", a=1)
                 .broadcast_to([128, 128]), loads)
            for k, name in enumerate(("Wq", "Wk", "Wv", "Wp")):
                load(wl1[:, k, :], ins[f"L1_conv_{name}"], loads)

            def turn_program(turn):
                a, c, d = turn.a, turn.c, turn.d
                if turn.active(3):
                    sp.wait_ge(*o_ready.after(a, 0))
                    sp.dma_start(out_view[:, bass.ds(a * TILES, 4), :], o_sb[:, :, :]).then_inc(stored.handle, 16)
                if turn.active(0) and turn.active(0, back=-1):
                    sp.wait_ge(*xp_ready.after(d, 1))
                    sp.dma_start(x_in[:, :, :], x_view[:, bass.ds((d + 1) * TILES, TILES), :]) \
                      .then_inc(x_loaded.handle, 16)
                if turn.active(1):
                    sp.wait_ge(*v_lo_ready.after(c, 1))
                    for dst, first, count_, src, tile in ((0, 1, 3, 96, 1), (64, 0, 4, 96, 0),
                                                          (32, 0, 4, 0, 1), (96, 0, 3, 0, 2)):
                        sp.dma_start(v_halo[dst:dst + 32, first:first + count_].bitcast(F32),
                                     v_hl[src:src + 32, tile:tile + 2 * count_ - 1:2].bitcast(F32)) \
                          .then_inc(halo_loaded.handle, 16)
                if turn.active(3):
                    sp.wait_ge(*o_ready.after(a, 1))
                    sp.dma_start(out_view[:, bass.ds(a * TILES + 4, 4), :], o_sb[:, :, :]).then_inc(stored.handle, 16)

            for it in (-3, -2, -1, 0):
                turn_program(Turn(it))
            with sp.Fori(1, B - 4) as i:
                turn_program(Turn(i))
            for it in (B - 4, B - 3, B - 2, B - 1):
                turn_program(Turn(it))
            sp.wait_ge(*stored.after(B - 1, 1))

        @block.tensor
        def _(te):
            def mm3(dst, w_pair, x_pair, first=True, last=True):
                (wh, wl), (xh, xl) = w_pair, x_pair
                te.matmul(dst, wh, xl, start=first, stop=False)
                te.matmul(dst, wl, xh, start=False, stop=False)
                return te.matmul(dst, wh, xh, start=False, stop=last)

            def xt(turn, k):
                n = turn.d
                te.wait_ge(*x_loaded.after(n, 0))
                te.wait_ge(*bank_free(turn, "xt", k))
                for t in range(4):
                    mm = te.transpose(bank("xt", k)[:, t * 128:(t + 1) * 128], x_in[:, 4 * k + t, :], ident)
                mm.then_inc(pe["xt"].handle, 1)

            def conv(turn, k):
                n, half, i = turn.c, k // 4, WINO[k % 4]
                te.wait_ge(*t_lo_ready.after(n, k // 2))
                te.wait_ge(*bank_free(turn, "conv", k))
                if turn.fixed and n == 0 and k < 4:
                    te.wait_ge(set_act, 1 + 3 * (k + 1))
                    te.wait_ge(set_pool, 1 + 3 * (k + 1))
                for m in range(2):
                    dst = bank("conv", k)[:, m * 256:(m + 1) * 256].rearrange("p (r w) -> p r w", r=PAIRS)
                    for dx in range(3):
                        xs = [t[:, i, :, dx:dx + W] for t in (t_hi, t_lo)]
                        ws = [wc[:, i, dx, m * 128:(m + 1) * 128] for wc in (wc_hi, wc_lo)]
                        mm = mm3(dst, ws, xs, dx == 0, dx == 2)
                mm.then_inc(pe["conv"].handle, 1)

            def up2(turn, half):
                n = turn.c
                te.wait_ge(*g_lo_ready.after(n, 2 * half + 1))
                te.wait_ge(*bank_free(turn, "up2", half))
                if turn.fixed and n == 0:
                    te.wait_ge(set_dve, 4)
                for m in range(2):
                    mm = mm3(bank("up2", half)[:, :], (w2_hi[:, m, :], w2_lo[:, m, :]),
                             (g_hi[:, m, :], g_lo[:, m, :]), m == 0, m == 1)
                mm.then_inc(pe["up2"].handle, 1)

            def project(turn, user, half, n, ready, w_pair, x_pair):
                te.wait_ge(*ready.after(n, half))
                te.wait_ge(*bank_free(turn, user, half))
                cols_ = slice(half * HALF, (half + 1) * HALF)
                mm3(bank(user, half)[:, :], w_pair, [x[:, cols_] for x in x_pair]) \
                    .then_inc(pe[user].handle, 1)

            def project_pixels(turn, user, half, n, ready, w_pair, x_pair):
                te.wait_ge(*ready.after(n, half))
                te.wait_ge(*bank_free(turn, user, half))
                for t in range(4):
                    pix = slice((4 * half + t) * 128, (4 * half + t + 1) * 128)
                    mm = mm3(bank(user, half)[:, t * 128:(t + 1) * 128], [x[:, pix] for x in x_pair], w_pair)
                mm.then_inc(pe[user].handle, 1)

            def q(turn, half):
                project(turn, "q", half, turn.c, h_lo_ready, (w0_hi[:, 0], w0_lo[:, 0]), (h_hi, h_lo))

            def k(turn, half):
                project(turn, "k", half, turn.c, h_lo_ready, (w0_hi[:, 1], w0_lo[:, 1]), (h_hi, h_lo))

            def v(turn, half):
                project_pixels(turn, "v", half, turn.c, h_lo_ready, (w0_hi[:, 2], w0_lo[:, 2]), (h_hi, h_lo))

            def local_scores(turn, j):
                n = turn.b
                te.wait_ge(*q_lo_ready.after(n, j // 2))
                te.wait_ge(*k_lo_ready.after(n, 1))
                te.wait_ge(*bank_free(turn, "as", j))
                for u in range(2):
                    t = 2 * j + u
                    dst = bank("as", j)[:, u * WIN:(u + 1) * WIN]
                    qs = [x[:, t * 128:(t + 1) * 128] for x in (q_hi, q_lo)]
                    ks = [x[:, 4 * t:4 * t + 6, :].rearrange("p r w -> p (r w)") for x in (kp_hi, kp_lo)]
                    mm = mm3(dst, qs, ks)
                mm.then_inc(pe["as"].handle, 1)

            def local_probs_t(turn, j):
                n = turn.b
                te.wait_ge(*p0n_ready.after(n, j))
                te.wait_ge(*bank_free(turn, "at", j))
                for u in range(2):
                    te.transpose(bank("at", j)[:, u * 128:(u + 1) * 128], pn_own[:, u, :], ident)
                for u in range(2):
                    mm = te.transpose(bank("at", j)[:, (2 + u) * 128:(3 + u) * 128],
                                      pn_halo[:, u * 128:(u + 1) * 128], ident)
                mm.then_inc(pe["at"].handle, 1)

            def local_values(turn, j):
                n = turn.b
                te.wait_ge(*pt_lo_ready.after(n, j))
                te.wait_ge(*halo_loaded.after(n, 3))
                te.wait_ge(*bank_free(turn, "av", j))
                mm3(bank("av", j)[:, 0:256], (v_halo[:, j, 0, :], v_halo[:, j, 1, :]),
                    [pt[:, 2:4, :].rearrange("p u c -> p (u c)") for pt in (pt_hi, pt_lo)], True, False)
                for u in range(2):
                    t = 2 * j + u
                    mm = mm3(bank("av", j)[:, u * 128:(u + 1) * 128], (v_hl[:, t, 0, :], v_hl[:, t, 1, :]),
                             (pt_hi[:, u, :], pt_lo[:, u, :]), False, u == 1)
                mm.then_inc(pe["av"].handle, 1)

            def group_moments(turn):
                n = turn.b
                te.wait_ge(*gn_step.after(n, 1))
                te.wait_ge(*bank_free(turn, "gn", 0))
                te.matmul(bank("gn", 0)[:, 0:2], group_avg, moments[:, :], start=True, stop=True) \
                  .then_inc(pe["gn"].handle, 1)

            def qq(turn, half):
                project(turn, "qq", half, turn.b, xn_lo_ready, (w1_hi[:, 0], w1_lo[:, 0]), (xn_hi, xn_lo))

            def kk(turn, half):
                project(turn, "kk", half, turn.b, xn_lo_ready, (w1_hi[:, 1], w1_lo[:, 1]), (xn_hi, xn_lo))

            def vv(turn, half):
                project_pixels(turn, "vv", half, turn.b, xn_lo_ready, (w1_hi[:, 2], w1_lo[:, 2]), (xn_hi, xn_lo))

            def residual_t(turn, half):
                n = turn.a
                te.wait_ge(*xb_ready.after(n, half))
                te.wait_ge(*bank_free(turn, "xbt", half))
                for t in range(4):
                    pix = slice((4 * half + t) * 128, (4 * half + t + 1) * 128)
                    mm = te.transpose(bank("xbt", half, n)[:, t * 128:(t + 1) * 128], y[:, pix], ident)
                mm.then_inc(pe["xbt"].handle, 1)

            def scores(n, t):
                te.wait_ge(*qq_lo_ready.after(n, t // 4))
                te.wait_ge(*kk_lo_ready.after(n, 1))
                if not is_last(n) or t == 0:
                    te.wait_ge(*e_ready.after(n, t - 1))
                elif t == 1:
                    te.wait_ge(*read_by(*Turn(B - 1).last_user(0)))
                    te.wait_ge(*read_by(*Turn(B - 1).last_user(1)))
                else:
                    te.wait_ge(*e_ready.after(n, t - 2))
                for half in range(2):
                    keys = slice(half * HALF, (half + 1) * HALF)
                    mm = mm3(score_tile(n, t)[:, keys], [x[:, t * 128:(t + 1) * 128] for x in (qq_hi, qq_lo)],
                             [x[:, keys] for x in (kk_hi, kk_lo)])
                mm.then_inc(pe["s"].handle, 1)

            def probs_t(n, t):
                te.wait_ge(*e_ready.after(n, t))
                te.wait_ge(*et_lo_ready.after(n, t - 1))
                for kt in range(TILES):
                    mm = te.transpose(ps_t[:, kt * 128:(kt + 1) * 128], e[:, kt * 128:(kt + 1) * 128], ident)
                mm.then_inc(pe["t"].handle, 1)

            def values(turn, j):
                n, cols_ = turn.a, slice((j % 2) * 256, (j % 2 + 1) * 256)
                te.wait_ge(*et_lo_ready.after(n, 2 * j + 1))
                te.wait_ge(*vv_lo_ready.after(n, 1))
                te.wait_ge(*bank_free(turn, "pv", j))
                for kt in range(TILES):
                    mm = mm3(bank("pv", j, n)[:, 0:256], (vv_hi[:, kt, :], vv_lo[:, kt, :]),
                             (et_hi[:, kt, cols_], et_lo[:, kt, cols_]), kt == 0, kt == TILES - 1)
                mm.then_inc(pe["pv"].handle, 1)

            def final_t(turn, half):
                n = turn.a
                te.wait_ge(*a_t_ready.after(n, 2 * half + 1))
                te.wait_ge(*bank_free(turn, "ft", half))
                for t in range(4):
                    mm = te.transpose(bank("ft", half, n)[:, t * 128:(t + 1) * 128], a_t[:, t * 128:(t + 1) * 128], ident)
                mm.then_inc(pe["ft"].handle, 1)

            te.wait_ge(loads_first, 16 * N_LOADS_FIRST)
            for j in range(3):
                for m in range(2):
                    dst = ps_s[:, (2 * j + m) * 128:(2 * j + m + 1) * 128]
                    mm = te.transpose(dst, w_up1[:, m, j:3 * C:3], ident)
            mm.then_inc(set_pe, 1)
            xt(Turn(-3), 0)
            xt(Turn(-3), 1)
            te.wait_ge(loads, 16 * N_LOADS)
            for m in range(2):
                te.transpose(ps_t[:, m * 128:(m + 1) * 128], w_up2[:, m * 128:(m + 1) * 128], ident)
            te.transpose(ps_t[:, 256:384], wl1[:, 2, :], ident).then_inc(set_pe, 1)
            for m in range(3):
                mm = te.transpose(ps_t[:, HALF + m * 128:HALF + (m + 1) * 128], w_qkv[:, m, :], ident)
            mm.then_inc(set_pe, 1)
            te.wait_ge(set_dve, 2)
            te.matmul(ps_s[:, 0:128], wv_t, wl1[:, 3, :], start=True, stop=True)
            te.matmul(ps_s[:, 128:129], wl1[:, 3, :], bv1, start=True, stop=True)
            for m in range(2):
                for j in range(3):
                    mm = te.matmul(ps_s[:, 129 + m:130 + m], w_up1_t[:, j, m * 128:(m + 1) * 128],
                                   b_perc[:, j:j + 1], start=(j == 0), stop=(j == 2))
            mm.then_inc(set_pe, 1)

            def turn_program(turn):
                p0, p1, p2, p3 = (turn.active(k) for k in range(4))
                a, b = turn.a, turn.b
                if p3:
                    residual_t(turn, 0)
                    residual_t(turn, 1)
                    scores(a, 1)
                if p2:
                    local_scores(turn, 0)
                if p3:
                    probs_t(a, 0)
                if p1:
                    conv(turn, 0)
                    conv(turn, 1)
                if p3:
                    scores(a, 2)
                    probs_t(a, 1)
                if p2:
                    local_probs_t(turn, 0)
                    local_scores(turn, 1)
                if p1:
                    conv(turn, 2)
                    conv(turn, 3)
                if p2 and p1:
                    local_values(turn, 0)
                if p3:
                    scores(a, 3)
                    probs_t(a, 2)
                if p2 and not p1:
                    local_values(turn, 0)
                if p2:
                    local_probs_t(turn, 1)
                    local_scores(turn, 2)
                if p1:
                    conv(turn, 4)
                    conv(turn, 5)
                if p2 and p1:
                    local_values(turn, 1)
                if p3:
                    scores(a, 4)
                    probs_t(a, 3)
                if p2 and not p1:
                    local_values(turn, 1)
                if p2:
                    local_probs_t(turn, 2)
                    local_scores(turn, 3)
                if p1:
                    up2(turn, 0)
                    conv(turn, 6)
                    conv(turn, 7)
                if p2:
                    local_values(turn, 2)
                if p2:
                    local_probs_t(turn, 3)
                if p3:
                    scores(a, 5)
                    values(turn, 0)
                    probs_t(a, 4)
                if p2:
                    local_values(turn, 3)
                if p1:
                    q(turn, 0)
                    k(turn, 0)
                    v(turn, 0)
                if p3:
                    scores(a, 6)
                if p2:
                    group_moments(turn)
                if p3:
                    probs_t(a, 5)
                if p1:
                    up2(turn, 1)
                if p3:
                    values(turn, 1)
                if p0:
                    xt(turn, 0)
                    xt(turn, 1)
                if p3:
                    scores(a, 7)
                    probs_t(a, 6)
                if p1:
                    q(turn, 1)
                    k(turn, 1)
                if p3:
                    final_t(turn, 0)
                    values(turn, 2)
                if p1:
                    v(turn, 1)
                if p2:
                    qq(turn, 0)
                if p3:
                    probs_t(a, 7)
                if p2:
                    kk(turn, 0)
                    qq(turn, 1)
                    kk(turn, 1)
                    vv(turn, 0)
                if p3:
                    values(turn, 3)
                if p2:
                    scores(b, 0)
                if p3:
                    final_t(turn, 1)
                if p2:
                    vv(turn, 1)

            run_turns(te, turn_program)

        @block.scalar
        def _(act):
            def t_hi_part(n, k):
                rows = T_PART[k % 2]
                act.wait_ge(*t_ready.after(n, k // 2))
                act.wait_ge(*pe["conv"].after(n, 2 * k - 3))
                act.activation(t_hi[:, rows], t_f[:, rows], ACT.Copy).then_inc(t_hi_ready.handle, 1)

            def take_m1(n, half):
                act.wait_ge(*pe["conv"].after(n, 4 * half))
                act.wait_ge(*g_ready.after(n, 2 * half - 1))
                act.activation(u[:, :, :, 0, :], bank("conv", 4 * half)[:, :]
                               .rearrange("p (m r w) -> p m r w", m=2, r=PAIRS), ACT.Copy).then_inc(u_step.handle, 1)

            def gelu(n, k, fixed):
                m = k % 2
                act.wait_ge(*u_step.after(n, 5 * (k // 2) + 4))
                if fixed and n == 0:
                    act.wait_ge(set_dve, 4)
                act.wait_ge(*g_lo_ready.after(n, k - 2))
                act.activation(g[:, m, :], u[:, m].rearrange("p r e w -> p (r e w)"), ACT.Gelu,
                               bias=b_hid[:, m:m + 1]).then_inc(g_ready.handle, 1)

            def h_hi_half(n, k):
                cols_ = slice(k * HALF, (k + 1) * HALF)
                act.wait_ge(*h_ready.after(n, k))
                act.wait_ge(*pe["v"].after(n - 1, 1))
                act.activation(h_hi[:, cols_], h[:, cols_], ACT.Copy).then_inc(h_hi_ready.handle, 1)

            def q_hi_half(n, k):
                act.wait_ge(*pe["q"].after(n, k))
                act.wait_ge(*pe["as"].after(n - 1, 3))
                act.activation(q_hi[:, k * HALF:(k + 1) * HALF], bank("q", k)[:, :], ACT.Identity, bias=bq0_s) \
                   .then_inc(q_hi_ready.handle, 1)

            def k_hi_half(n, k):
                act.wait_ge(*pe["k"].after(n, k))
                act.activation(kp_hi[:, 1 + k * ROWS:1 + (k + 1) * ROWS, 1:1 + W],
                               bank("k", k)[:, :].rearrange("p (r w) -> p r w", r=ROWS),
                               ACT.Identity, bias=b_qkv[:, 1:2]).then_inc(k_hi_ready.handle, 1)

            def v_hi_half(n, k):
                act.wait_ge(*v_ready.after(n, k))
                act.wait_ge(*pe["av"].after(n - 1, 3))
                act.activation(v_hl[:, 4 * k:4 * k + 4, 0, :], v_full[:, :, :], ACT.Copy) \
                   .then_inc(v_hi_ready.handle, 1)

            def local_exp(n, j):
                act.wait_ge(*max0_ready.after(n, j))
                for u in range(2):
                    t, tile = 2 * j + u, p0[:, 2 * (j % 2) + u]
                    ins_ = act.activation(tile, tile, ACT.Exp, bias=nm0[:, t:t + 1], accum_out=sum0[:, t:t + 1])
                ins_.then_inc(p0_ready.handle, 1)

            def pt_hi_pair(n, j):
                act.wait_ge(*pe["at"].after(n, j))
                act.wait_ge(*pe["av"].after(n, j - 1))
                act.activation(pt_hi[:, :, :], bank("at", j)[:, :].rearrange("p (u c) -> p u c", u=4), ACT.Copy) \
                   .then_inc(pt_hi_ready.handle, 1)

            def xn_hi_half(n, k):
                cols_ = slice(k * HALF, (k + 1) * HALF)
                act.wait_ge(*xn_ready.after(n, k))
                act.wait_ge(*pe["vv"].after(n - 1, 1))
                act.activation(xn_hi[:, cols_], y[:, cols_], ACT.Copy).then_inc(xn_hi_ready.handle, 1)

            def qq_hi_half(n, k):
                act.wait_ge(*pe["qq"].after(n, k))
                act.wait_ge(*pe["s"].after(n - 1, 7))
                act.activation(qq_hi[:, k * HALF:(k + 1) * HALF], bank("qq", k)[:, :], ACT.Identity, bias=bq1_s) \
                   .then_inc(qq_hi_ready.handle, 1)

            def kk_hi_half(n, k):
                act.wait_ge(*pe["kk"].after(n, k))
                act.activation(kk_hi[:, k * HALF:(k + 1) * HALF], bank("kk", k)[:, :], ACT.Identity, bias=bk1) \
                   .then_inc(kk_hi_ready.handle, 1)

            def vv_hi_half(n, k):
                act.wait_ge(*pe["vv"].after(n, k))
                act.wait_ge(*pe["pv"].after(n - 1, 3))
                act.activation(vv_hi[:, 4 * k:4 * k + 4, :], bank("vv", k)[:, :].rearrange("p (t c) -> p t c", t=4),
                               ACT.Copy).then_inc(vv_hi_ready.handle, 1)

            def residual(n, k):
                act.wait_ge(*pe["xbt"].after(n, k))
                act.wait_ge(*o_ready.after(n - 1, k))
                act.activation(r_tok[:, 4 * k:4 * k + 4, :], bank("xbt", k, n)[:, :].rearrange("p (t c) -> p t c", t=4),
                               ACT.Copy).then_inc(r_tok_ready.handle, 1)

            def exp(n, t):
                act.wait_ge(*max1_ready.after(n, t))
                act.wait_ge(*pe["t"].after(n, t - 1))
                if t % 4 == 0:
                    act.wait_ge(*rec1_ready.after(n - 1, t // 4))
                act.activation(e[:, :], score_tile(n, t)[:, :], ACT.Exp, bias=nm1[:, t:t + 1], accum_out=sum1[:, t:t + 1]) \
                   .then_inc(e_ready.handle, 1)

            def et_hi_tile(n, t):
                act.wait_ge(*pe["t"].after(n, t))
                if t % 2 == 0:
                    act.wait_ge(*pe["pv"].after(n, t // 2 - 2))
                act.activation(et_hi[:, :, (t % 4) * 128:(t % 4 + 1) * 128],
                               ps_t[:, :].rearrange("p (k c) -> p k c", k=TILES), ACT.Copy) \
                   .then_inc(et_hi_ready.handle, 1)

            def a_t_part(n, j):
                act.wait_ge(*pe["pv"].after(n, j))
                act.wait_ge(*pe["ft"].after(n, j // 2 - 1))
                act.activation(a_t[:, (j % 2) * 256:(j % 2 + 1) * 256], bank("pv", j, n)[:, 0:256], ACT.Copy) \
                   .then_inc(a_t_ready.handle, 1)

            def fold_first(k):
                i, dx = WINO[k // 3], k % 3
                if k >= 8:
                    act.wait_ge(set_pool, k - 6)
                act.activation(wc_f[k % 8], w_up1_t[:, 0, :], ACT.Copy, scale=wperc_g[:, 0, i, dx:dx + 1]) \
                   .then_inc(set_first, 1)

            act.dma_start(const[:, :], ins["const"]).then_inc(loads_first, 16)
            act.dma_start(wperc[:, :, :, :].rearrange("p j y x -> p (j y x)"),
                          ins["L0_conv_w_perc"].rearrange("(c j) a y x -> c (j a y x)", j=3)).then_inc(loads_first, 16)
            act.dma_start(cols[:, 0:15], ins["cols"]).then_inc(loads_first, 16)
            act.dma_start(w_up2, ins["L0_conv_w_up2"].rearrange("p f a b -> p (f a b)")).then_inc(loads, 16)
            act.wait_ge(loads_first, 16 * N_LOADS_FIRST)
            act.activation(bq0_s, b_qkv[:, 0:1], ACT.Copy, scale=SCALE)
            act.activation(bq1_s, bq1, ACT.Copy, scale=SCALE).then_inc(set_act, 1)
            act.wait_ge(set_dve, 1)
            for k in range(6):
                fold_first(k)
            for k in range(12):
                act.wait_ge(set_wc, k + 1)
                act.activation(wc_hi[:, WINO[k // 3], k % 3, :], wc_f[k % 8], ACT.Copy).then_inc(set_act, 1)
                if k == 2:
                    t_hi_part(0, 0)
                    t_hi_part(0, 1)
                if k + 6 < 12:
                    fold_first(k + 6)

            def turn_program(turn):
                p0, p1, p2, p3 = (turn.active(k) for k in range(4))
                a, b, c, d = turn.a, turn.b, turn.c, turn.d
                if p3:
                    residual(a, 0)
                    residual(a, 1)
                if p2:
                    local_exp(b, 0)
                if p3:
                    et_hi_tile(a, 0)
                    exp(a, 1)
                if p1:
                    take_m1(c, 0)
                if p3:
                    et_hi_tile(a, 1)
                if p2:
                    pt_hi_pair(b, 0)
                if p3:
                    exp(a, 2)
                if p2:
                    local_exp(b, 1)
                if p1:
                    t_hi_part(c, 2)
                    t_hi_part(c, 3)
                    gelu(c, 0, turn.fixed)
                    gelu(c, 1, turn.fixed)
                if p3:
                    et_hi_tile(a, 2)
                if p2:
                    pt_hi_pair(b, 1)
                if p3:
                    exp(a, 3)
                if p1:
                    take_m1(c, 1)
                if p2:
                    local_exp(b, 2)
                if p3:
                    et_hi_tile(a, 3)
                    exp(a, 4)
                if p2:
                    pt_hi_pair(b, 2)
                    local_exp(b, 3)
                if p1:
                    h_hi_half(c, 0)
                if p2:
                    pt_hi_pair(b, 3)
                if p1:
                    gelu(c, 2, turn.fixed)
                    gelu(c, 3, turn.fixed)
                if p3:
                    a_t_part(a, 0)
                    et_hi_tile(a, 4)
                    exp(a, 5)
                if p1:
                    q_hi_half(c, 0)
                    k_hi_half(c, 0)
                    v_hi_half(c, 0)
                if p3:
                    et_hi_tile(a, 5)
                    exp(a, 6)
                if p1:
                    h_hi_half(c, 1)
                if p2:
                    xn_hi_half(b, 0)
                    xn_hi_half(b, 1)
                if p3:
                    a_t_part(a, 1)
                if p3:
                    et_hi_tile(a, 6)
                    exp(a, 7)
                if p1:
                    q_hi_half(c, 1)
                    k_hi_half(c, 1)
                if p3:
                    a_t_part(a, 2)
                if p1:
                    v_hi_half(c, 1)
                if p2:
                    qq_hi_half(b, 0)
                if p3:
                    et_hi_tile(a, 7)
                if p2:
                    kk_hi_half(b, 0)
                    qq_hi_half(b, 1)
                    kk_hi_half(b, 1)
                if p0:
                    t_hi_part(d, 0)
                    t_hi_part(d, 1)
                if p3:
                    a_t_part(a, 3)
                if p2:
                    vv_hi_half(b, 0)
                    exp(b, 0)
                    vv_hi_half(b, 1)

            run_turns(act, turn_program)

        @block.gpsimd
        def _(pool):
            def minus(dst, full, hi):
                return pool.tensor_tensor(dst, full, hi, ALU.subtract)

            def transform(n, k):
                rows = [xp[:, k * ROWS + r:k * ROWS + r + ROWS - 1:2, :] for r in range(4)]
                pool.wait_ge(*xp_ready.after(n, 1))
                pool.wait_ge(*t_lo_ready.after(n, 2 * k - 1))
                for i, (x, y_, op) in enumerate(((0, 2, ALU.subtract), (1, 2, ALU.add), (2, 1, ALU.subtract),
                                                 (1, 3, ALU.subtract))):
                    ins_ = pool.tensor_tensor(t_f[:, i], rows[x], rows[y_], op)
                ins_.then_inc(t_ready.handle, 1)

            def t_lo_part(n, k):
                rows = T_PART[k % 2]
                pool.wait_ge(*t_hi_ready.after(n, k))
                minus(t_lo[:, rows], t_f[:, rows], t_hi[:, rows].bitcast(F32)).then_inc(t_lo_ready.handle, 1)

            def g_lo_part(n, k):
                pool.wait_ge(*g_hi_ready.after(n, k))
                minus(g_lo[:, k % 2, :], g[:, k % 2, :], g_hi[:, k % 2, :].bitcast(F32)) \
                    .then_inc(g_lo_ready.handle, 1)

            def h_lo_half(n, k):
                cols_ = slice(k * HALF, (k + 1) * HALF)
                pool.wait_ge(*h_hi_ready.after(n, k))
                minus(h_lo[:, cols_], h[:, cols_], h_hi[:, cols_].bitcast(F32)).then_inc(h_lo_ready.handle, 1)

            def v_lo_half(n, k):
                pool.wait_ge(*v_hi_ready.after(n, k))
                minus(v_hl[:, 4 * k:4 * k + 4, 1, :], v_full[:, :, :], v_hl[:, 4 * k:4 * k + 4, 0, :].bitcast(F32)) \
                    .then_inc(v_lo_ready.handle, 1)

            def xn_lo_half(n, k):
                cols_ = slice(k * HALF, (k + 1) * HALF)
                pool.wait_ge(*xn_hi_ready.after(n, k))
                minus(xn_lo[:, cols_], y[:, cols_], xn_hi[:, cols_].bitcast(F32)).then_inc(xn_lo_ready.handle, 1)

            pool.memset(xp[:, :, :], 0.0)
            for t in (kp_hi, kp_lo):
                pool.memset(t[:, :, :].bitcast(F32), 0.0)
            pool.memset(v_halo[:, :, :, :].bitcast(F32), 0.0)
            pool.memset(pn_halo[:, :], 0.0)
            pool.memset(minus_half[:, :], -0.5).then_inc(set_pool, 1)
            pool.wait_ge(set_pool, 1)
            transform(0, 0)
            for k in range(12):
                i, dx = WINO[k // 3], k % 3
                pool.wait_ge(set_act, k + 2)
                minus(wc_lo[:, i, dx, :], wc_f[k % 8], wc_hi[:, i, dx, :].bitcast(F32)).then_inc(set_pool, 1)
                if k == 2:
                    t_lo_part(0, 0)
                    t_lo_part(0, 1)

            def turn_program(turn):
                p0, p1, p2, p3 = (turn.active(k) for k in range(4))
                b, c, d = turn.b, turn.c, turn.d
                if p1:
                    transform(c, 1)
                    t_lo_part(c, 2)
                    t_lo_part(c, 3)
                    g_lo_part(c, 0)
                    g_lo_part(c, 1)
                    h_lo_half(c, 0)
                    g_lo_part(c, 2)
                    g_lo_part(c, 3)
                if p2:
                    pool.wait_ge(*gn_step.after(b, 4))
                    pool.tensor_tensor(rstd, var_eps, minus_half[:, :], ALU.pow).then_inc(rstd_ready.handle, 1)
                if p1:
                    v_lo_half(c, 0)
                    h_lo_half(c, 1)
                if p2:
                    xn_lo_half(b, 0)
                    xn_lo_half(b, 1)
                if p0:
                    transform(d, 0)
                    t_lo_part(d, 0)
                if p1:
                    v_lo_half(c, 1)
                if p0:
                    t_lo_part(d, 1)

            run_turns(pool, turn_program)

        @block.vector
        def _(dve):
            def x_half(n, k):
                dve.wait_ge(*pe["xt"].after(n, k))
                dve.wait_ge(*t_ready.after(n - 1, 1))
                dve.wait_ge(*h_ready.after(n - 1, 1))
                dve.tensor_copy(inside(xp, k), bank("xt", k)[:, :].rearrange("p (r w) -> p r w", r=ROWS)) \
                   .then_inc(xp_ready.handle, 1)

            own = ctx.enter_context(nc.semaphore("set_own"))
            done = [0]

            def step(ins_):
                ins_.then_inc(own, 1)
                done[0] += 1
                dve.wait_ge(own, done[0])

            def split(hi, lo, full):
                step(dve.tensor_copy(hi, full))
                dve.tensor_tensor(lo, full, hi.bitcast(F32), ALU.subtract)

            def other_weights():
                split(w2_hi[:, :, :], w2_lo[:, :, :], ps_t[:, 0:256].rearrange("p (m c) -> p m c", m=2))
                dve.wait_ge(set_pe, 3)
                step(dve.tensor_copy(w_qkv, ps_t[:, HALF:HALF + 384].rearrange("p (m c) -> p m c", m=3)))
                step(dve.tensor_scalar(w_qkv[:, 0, :], w_qkv[:, 0, :], SCALE, None, ALU.mult))
                split(w0_hi[:, :, :], w0_lo[:, :, :], w_qkv)
                step(dve.tensor_scalar(wl1[:, 0, :], wl1[:, 0, :], SCALE, None, ALU.mult))
                split(w1_hi[:, 0:2, :], w1_lo[:, 0:2, :], wl1[:, 0:2, :])
                dve.wait_ge(set_pe, 4)
                step(dve.tensor_copy(wvp, ps_s[:, 0:128]))
                split(w1_hi[:, 2, :], w1_lo[:, 2, :], wvp)
                dve.tensor_tensor(b_tot, ps_s[:, 128:129], bp1, ALU.add)
                dve.tensor_tensor(b_hid, ps_s[:, 129:131], b_up1, ALU.add).then_inc(set_dve, 1)
                dve.wait_ge(set_dve, 3)
                dve.wait_ge(set_act, 1)
                dve.memset(neg_var, 0.0).then_inc(set_dve, 1)

            def conv_rows(n, half, s, fixed):
                if fixed and n == 0 and (half, s) == (0, 4):
                    other_weights()
                pos, dst, src, op = ((1, 1, 0, ALU.subtract), (1, 0, 0, ALU.add), (2, 0, 0, ALU.add),
                                     (3, 1, 1, ALU.subtract))[s - 1]
                dve.wait_ge(*pe["conv"].after(n, 4 * half + pos))
                dve.wait_ge(*u_step.after(n, 5 * half + s - 1))
                dve.tensor_tensor(u[:, :, :, dst, :], u[:, :, :, src, :], bank("conv", 4 * half + pos)[:, :]
                                  .rearrange("p (m r w) -> p m r w", m=2, r=PAIRS), op).then_inc(u_step.handle, 1)

            def g_hi_part(n, k):
                dve.wait_ge(*g_ready.after(n, k))
                dve.wait_ge(*pe["up2"].after(n, k // 2 - 1))
                dve.tensor_copy(g_hi[:, k % 2, :], g[:, k % 2, :]).then_inc(g_hi_ready.handle, 1)

            def h_half(n, k):
                cols_ = slice(k * HALF, (k + 1) * HALF)
                dve.wait_ge(*pe["up2"].after(n, k))
                dve.wait_ge(*h_lo_ready.after(n - 1, k))
                dve.scalar_tensor_tensor(h[:, cols_].rearrange("p (r w) -> p r w", r=ROWS),
                                         bank("up2", k)[:, :].rearrange("p (r w) -> p r w", r=ROWS), b_up2,
                                         inside(xp, k), ALU.add, ALU.add) \
                   .then_inc(h_ready.handle, 1)

            def biased_lo(dst, src, bias, hi):
                return dve.scalar_tensor_tensor(dst, src, bias, hi, ALU.add, ALU.subtract)

            def q_lo_half(n, k):
                cols_ = slice(k * HALF, (k + 1) * HALF)
                dve.wait_ge(*q_hi_ready.after(n, k))
                biased_lo(q_lo[:, cols_], bank("q", k)[:, :], bq0_s, q_hi[:, cols_].bitcast(F32)) \
                    .then_inc(q_lo_ready.handle, 1)

            def k_lo_half(n, k):
                inside = (slice(None), slice(1 + k * ROWS, 1 + (k + 1) * ROWS), slice(1, 1 + W))
                dve.wait_ge(*k_hi_ready.after(n, k))
                biased_lo(kp_lo[inside], bank("k", k)[:, :].rearrange("p (r w) -> p r w", r=ROWS),
                          b_qkv[:, 1:2], kp_hi[inside].bitcast(F32)).then_inc(k_lo_ready.handle, 1)

            def v_half(n, k):
                dve.wait_ge(*pe["v"].after(n, k))
                dve.wait_ge(*v_lo_ready.after(n, k - 1))
                dve.tensor_tensor(v_full[:, :, :], bank("v", k)[:, :].rearrange("p (t c) -> p t c", t=4),
                                  bv0_row[:, :].rearrange("p (a c) -> p a c", a=1).broadcast_to([128, 4, 128]),
                                  ALU.add).then_inc(v_ready.handle, 1)

            def local_mask(n, j):
                dve.wait_ge(*pe["as"].after(n, j))
                dve.wait_ge(*p0n_ready.after(n, j - 2))
                dve.tensor_tensor(p0[:, 2 * (j % 2):2 * (j % 2) + 2].rearrange("p u r w -> p u (r w)"),
                                  bank("as", j)[:, 0:2 * WIN].rearrange("p (u k) -> p u k", u=2),
                                  mask.rearrange("p (a k) -> p a k", a=1).broadcast_to([128, 2, WIN]),
                                  ALU.add).then_inc(masked_ready.handle, 1)

            def local_max(n, j):
                dve.wait_ge(*masked_ready.after(n, j))
                dve.wait_ge(*p0_ready.after(n - 1, j))
                dve.tensor_reduce(nm0[:, 2 * j:2 * j + 2], p0[:, 2 * (j % 2):2 * (j % 2) + 2]
                                  .rearrange("p u r w -> p u (r w)"), AX.X, ALU.max, negate=True) \
                   .then_inc(max0_ready.handle, 1)

            def local_norm(n, j):
                dve.wait_ge(*p0_ready.after(n, j))
                dve.reciprocal(rec0[:, 2 * j:2 * j + 2], sum0[:, 2 * j:2 * j + 2]).then_inc(rec0_ready.handle, 1)
                dve.wait_ge(*rec0_ready.after(n, j))
                dve.wait_ge(*pe["at"].after(n, j - 1))
                pair = p0[:, 2 * (j % 2):2 * (j % 2) + 2]
                rec = rec0[:, 2 * j:2 * j + 2].rearrange("p (u r w) -> p u r w", r=1, w=1)
                dve.tensor_tensor(pn_own[:, :, :].rearrange("p u (r w) -> p u r w", r=4), pair[:, :, 1:5, 1:1 + W],
                                  rec.broadcast_to([128, 2, 4, W]), ALU.mult)
                halo = pn_halo[:, :].rearrange("p (u x) -> p u x", u=2)[:, :, 0:64].rearrange("p u (r w) -> p u r w", r=2)
                ins_ = dve.tensor_tensor(halo, pair[:, :, 0:6:5, 1:1 + W], rec.broadcast_to([128, 2, 2, W]), ALU.mult)
                ins_.then_inc(p0n_ready.handle, 1)

            def pt_lo_pair(n, j):
                dve.wait_ge(*pt_hi_ready.after(n, j))
                dve.tensor_tensor(pt_lo[:, :, :], bank("at", j)[:, :].rearrange("p (u c) -> p u c", u=4),
                                  pt_hi[:, :, :].bitcast(F32), ALU.subtract).then_inc(pt_lo_ready.handle, 1)

            def y_pair(n, j):
                cols_ = slice(j * 256, (j + 1) * 256)
                dve.wait_ge(*pe["av"].after(n, j))
                dve.wait_ge(*pe["xbt"].after(n - 1, j // 2))
                dve.tensor_tensor(y[:, cols_], bank("av", j)[:, 0:256], h[:, cols_], ALU.add) \
                   .then_inc(y_ready.handle, 1)
                dve.wait_ge(*y_ready.after(n, j))
                dve.bn_stats(stats[:, j, :], y[:, cols_]).then_inc(stat_ready.handle, 1)

            def channel_moments(n):
                dve.bn_aggr(moments[:, :], stats[:, :, :].rearrange("p a s -> p (a s)")).then_inc(gn_step.handle, 1)
                dve.wait_ge(*gn_step.after(n, 0))
                dve.scalar_tensor_tensor(moments[:, 1:2], moments[:, 0:1], moments[:, 0:1], moments[:, 1:2],
                                         ALU.mult, ALU.add).then_inc(gn_step.handle, 1)

            def group_variance(n):
                dve.wait_ge(*pe["gn"].after(n, 0))
                dve.tensor_copy(g_mom[:, :], bank("gn", 0)[:, 0:2]).then_inc(gn_step.handle, 1)
                dve.wait_ge(*gn_step.after(n, 2))
                dve.scalar_tensor_tensor(neg_var, g_mom[:, 0:1], g_mom[:, 0:1], g_mom[:, 1:2],
                                         ALU.mult, ALU.subtract).then_inc(gn_step.handle, 1)
                dve.wait_ge(*gn_step.after(n, 3))
                dve.tensor_scalar(var_eps, neg_var, -1.0, EPS, ALU.mult, ALU.add).then_inc(gn_step.handle, 1)

            def group_norm(n):
                dve.wait_ge(*rstd_ready.after(n, 0))
                dve.tensor_tensor(gn_a, gamma, rstd, ALU.mult).then_inc(gn_step.handle, 1)
                dve.wait_ge(*gn_step.after(n, 5))
                dve.scalar_tensor_tensor(gn_nb, g_mom[:, 0:1], gn_a, beta, ALU.mult, ALU.subtract) \
                   .then_inc(gn_step.handle, 1)
                dve.wait_ge(*gn_step.after(n, 6))
                for k in range(2):
                    cols_ = slice(k * HALF, (k + 1) * HALF)
                    dve.tensor_scalar(y[:, cols_], y[:, cols_], gn_a, gn_nb, ALU.mult, ALU.subtract) \
                       .then_inc(xn_ready.handle, 1)

            def residual_bias(n, k):
                cols_ = slice(k * HALF, (k + 1) * HALF)
                dve.wait_ge(*xn_lo_ready.after(n, k))
                dve.tensor_scalar(y[:, cols_], y[:, cols_], b_tot, None, ALU.add).then_inc(xb_ready.handle, 1)

            def qq_lo_half(n, k):
                cols_ = slice(k * HALF, (k + 1) * HALF)
                dve.wait_ge(*qq_hi_ready.after(n, k))
                biased_lo(qq_lo[:, cols_], bank("qq", k)[:, :], bq1_s, qq_hi[:, cols_].bitcast(F32)) \
                    .then_inc(qq_lo_ready.handle, 1)

            def kk_lo_half(n, k):
                cols_ = slice(k * HALF, (k + 1) * HALF)
                dve.wait_ge(*kk_hi_ready.after(n, k))
                biased_lo(kk_lo[:, cols_], bank("kk", k)[:, :], bk1, kk_hi[:, cols_].bitcast(F32)) \
                    .then_inc(kk_lo_ready.handle, 1)

            def vv_lo_half(n, k):
                dve.wait_ge(*vv_hi_ready.after(n, k))
                dve.tensor_tensor(vv_lo[:, 4 * k:4 * k + 4, :], bank("vv", k)[:, :].rearrange("p (t c) -> p t c", t=4),
                                  vv_hi[:, 4 * k:4 * k + 4, :].bitcast(F32), ALU.subtract) \
                   .then_inc(vv_lo_ready.handle, 1)

            def row_max(n, t):
                dve.wait_ge(*pe["s"].after(n, t))
                dve.wait_ge(*e_ready.after(n - 1, t))
                dve.tensor_reduce(nm1[:, t:t + 1], score_tile(n, t)[:, :], AX.X, ALU.max, negate=True) \
                   .then_inc(max1_ready.handle, 1)

            def et_lo_tile(n, t):
                cols_ = slice((t % 4) * 128, (t % 4 + 1) * 128)
                dve.wait_ge(*et_hi_ready.after(n, t))
                dve.tensor_tensor(et_lo[:, :, cols_], ps_t[:, :].rearrange("p (k c) -> p k c", k=TILES),
                                  et_hi[:, :, cols_].bitcast(F32), ALU.subtract).then_inc(et_lo_ready.handle, 1)

            def output(n, k):
                four = slice(4 * k, 4 * k + 4)
                dve.wait_ge(*e_ready.after(n, 4 * k + 3))
                dve.reciprocal(rec1[:, four], sum1[:, four]).then_inc(rec1_ready.handle, 1)
                dve.wait_ge(*rec1_ready.after(n, k))
                dve.wait_ge(*pe["ft"].after(n, k))
                dve.wait_ge(*r_tok_ready.after(n, k))
                dve.wait_ge(*stored.after(n, k - 1))
                for t in range(4):
                    ins_ = dve.scalar_tensor_tensor(o_sb[:, t, :], bank("ft", k, n)[:, t * 128:(t + 1) * 128],
                                                    rec1[:, 4 * k + t:4 * k + t + 1], r_tok[:, 4 * k + t, :],
                                                    ALU.mult, ALU.add)
                ins_.then_inc(o_ready.handle, 1)

            dve.wait_ge(loads_first, 16 * N_LOADS_FIRST)
            step(dve.tensor_copy(wperc_g[:, :, 0:4:3, :], wperc[:, :, 0:3:2, :]))
            step(dve.tensor_tensor(wperc_g[:, :, 1, :], wperc[:, :, 0, :], wperc[:, :, 2, :], ALU.add))
            step(dve.tensor_tensor(wperc_g[:, :, 2, :], wperc_g[:, :, 1, :], wperc[:, :, 1, :], ALU.subtract))
            step(dve.tensor_tensor(wperc_g[:, :, 1, :], wperc_g[:, :, 1, :], wperc[:, :, 1, :], ALU.add))
            step(dve.tensor_scalar(wperc_g[:, :, 1:3, :], wperc_g[:, :, 1:3, :], 0.5, None, ALU.mult))
            dve.wait_ge(set_pe, 1)
            dve.tensor_copy(w_up1_t, ps_s[:, 0:768].rearrange("p (j d) -> p j d", j=3)).then_inc(set_dve, 1)
            dve.wait_ge(set_pool, 1)
            x_half(0, 0)
            x_half(0, 1)
            dve.wait_ge(set_pe, 2)
            dve.tensor_copy(wv_t, ps_t[:, 256:384]).then_inc(set_dve, 1)
            dve.wait_ge(set_dve, 2)
            for k in range(12):
                i, dx = WINO[k // 3], k % 3
                acc = wc_f[k % 8]
                dve.wait_ge(set_first, k + 1)
                step(dve.scalar_tensor_tensor(acc, w_up1_t[:, 1, :], wperc_g[:, 1, i, dx:dx + 1], acc, ALU.mult, ALU.add))
                dve.scalar_tensor_tensor(acc, w_up1_t[:, 2, :], wperc_g[:, 2, i, dx:dx + 1], acc, ALU.mult, ALU.add) \
                   .then_inc(set_wc, 1)

            def turn_program(turn):
                p0, p1, p2, p3 = (turn.active(k) for k in range(4))
                a, b, c, d = turn.a, turn.b, turn.c, turn.d
                if p2:
                    local_mask(b, 0)
                    local_max(b, 0)
                if p3:
                    row_max(a, 1)
                if p2:
                    local_norm(b, 0)
                if p3:
                    et_lo_tile(a, 0)
                if p1:
                    conv_rows(c, 0, 1, turn.fixed)
                    conv_rows(c, 0, 2, turn.fixed)
                if p3:
                    row_max(a, 2)
                    et_lo_tile(a, 1)
                if p2:
                    local_mask(b, 1)
                    local_max(b, 1)
                    pt_lo_pair(b, 0)
                if p1:
                    conv_rows(c, 0, 3, turn.fixed)
                if p2:
                    local_norm(b, 1)
                if p1:
                    conv_rows(c, 0, 4, turn.fixed)
                if p2 and p1:
                    y_pair(b, 0)
                if p3:
                    row_max(a, 3)
                if p1:
                    g_hi_part(c, 0)
                    g_hi_part(c, 1)
                if p2:
                    local_mask(b, 2)
                    local_max(b, 2)
                if p3:
                    et_lo_tile(a, 2)
                if p2 and not p1:
                    y_pair(b, 0)
                if p2:
                    pt_lo_pair(b, 1)
                if p1:
                    conv_rows(c, 1, 1, turn.fixed)
                if p2:
                    local_norm(b, 2)
                if p1:
                    conv_rows(c, 1, 2, turn.fixed)
                if p2 and p1:
                    y_pair(b, 1)
                if p3:
                    row_max(a, 4)
                    et_lo_tile(a, 3)
                if p2 and not p1:
                    y_pair(b, 1)
                if p2:
                    local_mask(b, 3)
                    local_max(b, 3)
                    pt_lo_pair(b, 2)
                if p1:
                    h_half(c, 0)
                if p2:
                    local_norm(b, 3)
                if p1:
                    conv_rows(c, 1, 3, turn.fixed)
                    conv_rows(c, 1, 4, turn.fixed)
                if p2:
                    y_pair(b, 2)
                    pt_lo_pair(b, 3)
                if p3:
                    row_max(a, 5)
                if p1:
                    g_hi_part(c, 2)
                if p3:
                    et_lo_tile(a, 4)
                if p2:
                    y_pair(b, 3)
                    dve.wait_ge(*stat_ready.after(b, 3))
                if p1:
                    g_hi_part(c, 3)
                if p2:
                    channel_moments(b)
                if p1:
                    q_lo_half(c, 0)
                    k_lo_half(c, 0)
                    v_half(c, 0)
                if p3:
                    row_max(a, 6)
                if p2:
                    group_variance(b)
                    group_norm(b)
                if p1:
                    h_half(c, 1)
                if p3:
                    et_lo_tile(a, 5)
                if p0:
                    x_half(d, 0)
                    x_half(d, 1)
                if p3:
                    row_max(a, 7)
                    et_lo_tile(a, 6)
                if p1:
                    q_lo_half(c, 1)
                    k_lo_half(c, 1)
                if p3:
                    output(a, 0)
                if p1:
                    v_half(c, 1)
                if p2:
                    qq_lo_half(b, 0)
                if p3:
                    et_lo_tile(a, 7)
                if p2:
                    qq_lo_half(b, 1)
                    kk_lo_half(b, 0)
                    kk_lo_half(b, 1)
                    residual_bias(b, 0)
                    residual_bias(b, 1)
                    row_max(b, 0)
                    vv_lo_half(b, 0)
                if p3:
                    output(a, 1)
                if p2:
                    vv_lo_half(b, 1)

            run_turns(dve, turn_program)


_INS = ["x", "L0_conv_w_perc", "L0_conv_w_up1", "L0_conv_w_up2", "L0_conv_w_qkv", "L0_conv_b_qkv",
        "L1_conv_Wq", "L1_conv_Wk", "L1_conv_Wv", "L1_conv_Wp"]
_COLS = [("L0_conv_b_perc", 3), ("L0_conv_b_up1", 2), ("L0_conv_b_up2", 1), ("L0_conv_b_qkv", 3), ("L1_conv_gamma", 1),
         ("L1_conv_beta", 1), ("L1_conv_bq", 1), ("L1_conv_bk", 1), ("L1_conv_bv", 1), ("L1_conv_bp", 1)]


def kernel(**inputs):
    import numpy as np
    import concourse.bacc as bacc
    from concourse.bass_utils import run_bass_kernel_spmd

    const = np.zeros((128, CONST_W), np.float32)
    const[:, 0:128] = np.eye(128)
    row, col = np.arange(128) // W, np.arange(128) % W
    key_row, key_col = np.arange(WIN) // WP, np.arange(WIN) % WP
    dy, dx = key_row[None] - row[:, None], key_col[None] - col[:, None]
    const[:, 128:128 + WIN] = np.where((dy >= 0) & (dy <= 2) & (dx >= 0) & (dx <= 2), 0.0, MASKED)
    groups = np.arange(128) // GROUP
    const[:, 128 + WIN:] = (groups[:, None] == groups[None]) / GROUP

    nc = bacc.Bacc("TRN2", target_bir_lowering=False, num_devices=1)
    arrays, views = {}, {}
    cols = [np.asarray(inputs[name]).reshape(128, k) if name == "L0_conv_b_perc"
            else np.asarray(inputs[name]).reshape(k, 128).T for name, k in _COLS]
    extra = {"const": const, "cols": np.ascontiguousarray(np.concatenate(cols, axis=1))}
    for name in _INS + ["const", "cols"]:
        array = extra[name] if name in extra else np.ascontiguousarray(inputs[name])
        arrays[f"in_{name}"] = array
        views[name] = nc.dram_tensor(f"in_{name}", array.shape, mybir.dt.from_np(array.dtype), kind="ExternalInput").ap()
    out = nc.dram_tensor("out", (B, H, W, C), F32, kind="ExternalOutput").ap()
    conv_seq_kernel(nc, views, out)
    result = run_bass_kernel_spmd(nc, [arrays], core_ids=[0])
    return result.results[0]["out"]
```
